# Optimizing a Trainium2 kernel written in Bass

```python
import numpy as np
import jax
import jax.numpy as jnp

def _softmax(x, axis=-1):
    return jax.nn.softmax(x, axis=axis)

def _gelu(x):
    return jax.nn.gelu(x, approximate=True)

def _silu(x):
    return jax.nn.silu(x)

def _sigmoid(x):
    return jax.nn.sigmoid(x)

def _layernorm(x, axis=-1, eps=1e-05):
    m = jnp.mean(x, axis=axis, keepdims=True)
    v = jnp.var(x, axis=axis, keepdims=True)
    return (x - m) / jnp.sqrt(v + eps)

def _scatter_add(tgt, idx, src, axis=0):
    return tgt.at[idx].add(src)

def _segment_sum(src, seg, n):
    return jax.ops.segment_sum(src, seg, n)
kernel_name = 'mk_adaln_d2_jaxref_r8_bb7436'

def setup_inputs(seed: int=0):
    np.random.seed(seed)
    _w = jnp.asarray

    def _L0_attn_setup():
        import jax, jax.numpy as jnp
        import numpy as np
        B, N, D, H = (8, 512, 128, 16)
        HD = D // H
        EPS = 1e-05
        key = jax.random.key(seed)
        ks = jax.random.split(key, 18)
        s = 1.0 / np.sqrt(D)

        def lin(k):
            return (jax.random.normal(k, (D, D), jnp.float32) * s, jnp.zeros((D,), jnp.float32))
        Wg_w, Wg_b = lin(ks[0])
        Wr_w, Wr_b = lin(ks[1])
        Wk_w, Wk_b = lin(ks[2])
        Wv_w, Wv_b = lin(ks[3])
        Wo_w, Wo_b = lin(ks[4])
        mg = jax.random.uniform(ks[5], (D,), jnp.float32)
        mr = jax.random.uniform(ks[6], (D,), jnp.float32)
        mk = jax.random.uniform(ks[7], (D,), jnp.float32)
        mv = jax.random.uniform(ks[8], (D,), jnp.float32)
        w = jax.random.normal(ks[9], (H, HD), jnp.float32)
        u = jax.random.normal(ks[10], (H, HD), jnp.float32)
        x = jax.random.normal(ks[11], (B, N, D), jnp.float32)
        return {'x': x, 'Wg_w': Wg_w, 'Wg_b': Wg_b, 'Wr_w': Wr_w, 'Wr_b': Wr_b, 'Wk_w': Wk_w, 'Wk_b': Wk_b, 'Wv_w': Wv_w, 'Wv_b': Wv_b, 'Wo_w': Wo_w, 'Wo_b': Wo_b, 'mg': mg, 'mr': mr, 'mk': mk, 'mv': mv, 'w': w, 'u': u}
    _L0_attn_in = _L0_attn_setup()

    def _L0_ffn_setup():
        import jax, jax.numpy as jnp
        import numpy as np
        DIM = 128
        DEPTH = 6
        HEADS = 16
        DIM_HEAD = 64
        WINDOW = 32
        INNER = HEADS * DIM_HEAD
        DIM_INNER = int(DIM * 4 * 2 / 3)
        QK_SCALE = 8.0

        def shift_tokens(t):
            a, s = jnp.split(t, 2, -1)
            s = jnp.pad(s, ((0, 0), (1, 0), (0, 0)))[:, :-1]
            return jnp.concatenate([a, s], -1)

        def l2norm(t):
            return t / jnp.maximum(jnp.linalg.norm(t, axis=-1, keepdims=True), 1e-12)

        def rotate_half(x):
            x1, x2 = jnp.split(x, 2, -1)
            return jnp.concatenate([-x2, x1], -1)

        def rotary_tables(n):
            half = jnp.arange(0, DIM_HEAD, 2, dtype=jnp.float32)
            inv_freq = 1.0 / 10000.0 ** (half / DIM_HEAD)
            t = jnp.arange(n, dtype=jnp.float32)
            freqs = t[:, None] * inv_freq[None, :]
            freqs = jnp.concatenate([freqs, freqs], -1)
            base_scale = (half + 0.4 * DIM_HEAD) / (1.4 * DIM_HEAD)
            power = (t - n // 2) / (WINDOW // 2)
            scale = base_scale[None, :] ** power[:, None]
            scale = jnp.concatenate([scale, scale], -1)
            return (freqs, scale)

        def local_attention(q, k, v):
            b, h, n, d = q.shape
            w = WINDOW
            nw = n // w
            bq = q.reshape(b, h, nw, w, d)
            bk = k.reshape(b, h, nw, w, d)
            bv = v.reshape(b, h, nw, w, d)

            def look(t):
                p = jnp.pad(t, ((0, 0), (0, 0), (1, 0), (0, 0), (0, 0)))
                return jnp.concatenate([p[:, :, :nw], p[:, :, 1:]], axis=3)
            bk2, bv2 = (look(bk), look(bv))
            seq = jnp.arange(n).reshape(nw, w)
            seq_p = jnp.pad(seq, ((1, 0), (0, 0)), constant_values=-1)
            jt = jnp.concatenate([seq_p[:nw], seq_p[1:]], axis=1)
            it = seq[:, :, None]
            jb = jt[:, None, :]
            mask = (it < jb) | (it > jb + w) | (jb == -1)
            sim = jnp.einsum('bhwie,bhwje->bhwij', bq, bk2) * QK_SCALE
            sim = jnp.where(mask, -jnp.finfo(sim.dtype).max, sim)
            attn = jax.nn.softmax(sim, -1)
            out = jnp.einsum('bhwij,bhwje->bhwie', attn, bv2)
            return out.reshape(b, h, n, d)

        def attn_layer(x, Wqkv, qs, ksc, Wo):
            b, n, _ = x.shape
            qkv = x @ Wqkv
            q, k, v = jnp.split(qkv, 3, -1)
            sh = lambda t: t.reshape(b, n, HEADS, DIM_HEAD).transpose(0, 2, 1, 3)
            q, k, v = (sh(q), sh(k), sh(v))
            q = l2norm(q) * qs
            k = l2norm(k) * ksc
            freqs, scale = rotary_tables(n)
            cos, sin = (jnp.cos(freqs), jnp.sin(freqs))
            q = q * cos * scale + rotate_half(q) * sin * scale
            inv = 1.0 / scale
            k = k * cos * inv + rotate_half(k) * sin * inv
            out = local_attention(q, k, v)
            out = out.transpose(0, 2, 1, 3).reshape(b, n, INNER)
            return out @ Wo

        def ffn_layer(x, g, bln, W1, b1, W2, b2):
            mu = x.mean(-1, keepdims=True)
            var = ((x - mu) ** 2).mean(-1, keepdims=True)
            xn = (x - mu) / jnp.sqrt(var + 1e-05) * g + bln
            hg = xn @ W1 + b1
            a, gate = jnp.split(hg, 2, -1)
            return a * jax.nn.gelu(gate, approximate=False) @ W2 + b2
        key = jax.random.key(seed)
        ks = jax.random.split(key, 8)
        B, N = (2, 256)
        init = lambda k, shape: jax.random.normal(k, shape, jnp.float32) * 0.02
        return {'x': jax.random.normal(ks[0], (B, N, DIM), jnp.float32), 'Wqkv': init(ks[1], (DEPTH, DIM, 3 * INNER)), 'q_scale': jnp.ones((DEPTH, DIM_HEAD), jnp.float32), 'k_scale': jnp.ones((DEPTH, DIM_HEAD), jnp.float32), 'Wo': init(ks[2], (DEPTH, INNER, DIM)), 'ln_g': jnp.ones((DEPTH, DIM), jnp.float32), 'ln_b': jnp.zeros((DEPTH, DIM), jnp.float32), 'W1': init(ks[3], (DEPTH, DIM, 2 * DIM_INNER)), 'b1': jnp.zeros((DEPTH, 2 * DIM_INNER), jnp.float32), 'W2': init(ks[4], (DEPTH, DIM_INNER, DIM)), 'b2': jnp.zeros((DEPTH, DIM), jnp.float32)}
    _L0_ffn_in = _L0_ffn_setup()
    _L0_c = _w((lambda *s: np.random.randn(*s).astype(np.float32) * 0.05)(2, 128))
    _L0_wmod = _w((lambda *s: np.random.randn(*s).astype(np.float32) * 0.05)(128, 6 * 128) * 128 ** (-0.5))

    def _L1_attn_setup():
        import jax, jax.numpy as jnp
        import numpy as np
        HEADS = 16
        DIM_HEAD = 64
        key = jax.random.key(seed)
        k1, k2, k3, k4 = jax.random.split(key, 4)
        B, T, D = (4, 128, 128)
        x = jax.random.normal(k1, (B, T, D), dtype=jnp.float32)
        w_qkv = jax.random.normal(k2, (3 * HEADS * DIM_HEAD, D), dtype=jnp.float32) * (1.0 / np.sqrt(D))
        w_out = jax.random.normal(k3, (D, HEADS * DIM_HEAD), dtype=jnp.float32) * (1.0 / np.sqrt(HEADS * DIM_HEAD))
        rel_bias = jax.random.normal(k4, (2 * 128 - 1, HEADS), dtype=jnp.float32) * 0.02
        return {'x': x, 'w_qkv': w_qkv, 'w_out': w_out, 'rel_bias': rel_bias}
    _L1_attn_in = _L1_attn_setup()

    def _L1_ffn_setup():
        import jax, jax.numpy as jnp
        import numpy as np
        TOP_K = 2
        key = jax.random.key(seed)
        ks = jax.random.split(key, 4)
        B, S, D, E, F = (4, 256, 128, 8, 512)
        x = jax.random.normal(ks[0], (B, S, D), dtype=jnp.float32)
        gate_w = jax.random.normal(ks[1], (D, E), dtype=jnp.float32) * (1.0 / np.sqrt(D))
        w1 = jax.random.normal(ks[2], (E, D, F), dtype=jnp.float32) * (1.0 / np.sqrt(D))
        b1 = jnp.zeros((E, F), dtype=jnp.float32)
        w2 = jax.random.normal(ks[3], (E, F, D), dtype=jnp.float32) * (1.0 / np.sqrt(F))
        b2 = jnp.zeros((E, D), dtype=jnp.float32)
        return {'x': x, 'gate_w': gate_w, 'w1': w1, 'b1': b1, 'w2': w2, 'b2': b2}
    _L1_ffn_in = _L1_ffn_setup()
    _L1_c = _w((lambda *s: np.random.randn(*s).astype(np.float32) * 0.05)(2, 128))
    _L1_wmod = _w((lambda *s: np.random.randn(*s).astype(np.float32) * 0.05)(128, 6 * 128) * 128 ** (-0.5))
    _d = {'L0_attn_x': _L0_attn_in['x'], 'L0_attn_Wg_w': _L0_attn_in['Wg_w'], 'L0_attn_Wg_b': _L0_attn_in['Wg_b'], 'L0_attn_Wr_w': _L0_attn_in['Wr_w'], 'L0_attn_Wr_b': _L0_attn_in['Wr_b'], 'L0_attn_Wk_w': _L0_attn_in['Wk_w'], 'L0_attn_Wk_b': _L0_attn_in['Wk_b'], 'L0_attn_Wv_w': _L0_attn_in['Wv_w'], 'L0_attn_Wv_b': _L0_attn_in['Wv_b'], 'L0_attn_Wo_w': _L0_attn_in['Wo_w'], 'L0_attn_Wo_b': _L0_attn_in['Wo_b'], 'L0_attn_mg': _L0_attn_in['mg'], 'L0_attn_mr': _L0_attn_in['mr'], 'L0_attn_mk': _L0_attn_in['mk'], 'L0_attn_mv': _L0_attn_in['mv'], 'L0_attn_w': _L0_attn_in['w'], 'L0_attn_u': _L0_attn_in['u'], 'L0_ffn_Wqkv': _L0_ffn_in['Wqkv'], 'L0_ffn_q_scale': _L0_ffn_in['q_scale'], 'L0_ffn_k_scale': _L0_ffn_in['k_scale'], 'L0_ffn_Wo': _L0_ffn_in['Wo'], 'L0_ffn_ln_g': _L0_ffn_in['ln_g'], 'L0_ffn_ln_b': _L0_ffn_in['ln_b'], 'L0_ffn_W1': _L0_ffn_in['W1'], 'L0_ffn_b1': _L0_ffn_in['b1'], 'L0_ffn_W2': _L0_ffn_in['W2'], 'L0_ffn_b2': _L0_ffn_in['b2'], 'L0_c': _L0_c, 'L0_wmod': _L0_wmod, 'L1_attn_w_qkv': _L1_attn_in['w_qkv'], 'L1_attn_w_out': _L1_attn_in['w_out'], 'L1_attn_rel_bias': _L1_attn_in['rel_bias'], 'L1_ffn_gate_w': _L1_ffn_in['gate_w'], 'L1_ffn_w1': _L1_ffn_in['w1'], 'L1_ffn_b1': _L1_ffn_in['b1'], 'L1_ffn_w2': _L1_ffn_in['w2'], 'L1_ffn_b2': _L1_ffn_in['b2'], 'L1_c': _L1_c, 'L1_wmod': _L1_wmod}
    _x0 = _d['L0_attn_x']
    _d['L0_attn_x'] = jax.random.normal(jax.random.fold_in(jax.random.key(seed), 1), (2, 1024, 128), dtype=_x0.dtype)
    del _x0
    return _d

def reference(L0_attn_x, L0_attn_Wg_w, L0_attn_Wg_b, L0_attn_Wr_w, L0_attn_Wr_b, L0_attn_Wk_w, L0_attn_Wk_b, L0_attn_Wv_w, L0_attn_Wv_b, L0_attn_Wo_w, L0_attn_Wo_b, L0_attn_mg, L0_attn_mr, L0_attn_mk, L0_attn_mv, L0_attn_w, L0_attn_u, L0_ffn_Wqkv, L0_ffn_q_scale, L0_ffn_k_scale, L0_ffn_Wo, L0_ffn_ln_g, L0_ffn_ln_b, L0_ffn_W1, L0_ffn_b1, L0_ffn_W2, L0_ffn_b2, L0_c, L0_wmod, L1_attn_w_qkv, L1_attn_w_out, L1_attn_rel_bias, L1_ffn_gate_w, L1_ffn_w1, L1_ffn_b1, L1_ffn_w2, L1_ffn_b2, L1_c, L1_wmod):

    def _L0_attn_ref(x, Wg_w, Wg_b, Wr_w, Wr_b, Wk_w, Wk_b, Wv_w, Wv_b, Wo_w, Wo_b, mg, mr, mk, mv, w, u):
        import jax, jax.numpy as jnp
        import numpy as np
        B, N, D, H = (8, 512, 128, 16)
        HD = D // H
        EPS = 1e-05
        b, n, d = x.shape
        x_shift = jnp.roll(x, shift=1, axis=1)

        def mix(m, W, bias):
            return (m * x + (1.0 - m) * x_shift) @ W.T + bias
        g = mix(mg, Wg_w, Wg_b).reshape(b, n, H, HD)
        r = mix(mr, Wr_w, Wr_b).reshape(b, n, H, HD)
        k = mix(mk, Wk_w, Wk_b).reshape(b, n, H, HD)
        v = mix(mv, Wv_w, Wv_b).reshape(b, n, H, HD)
        kv = k * v
        decay = jnp.exp(-jnp.exp(w))
        kv_t = jnp.swapaxes(kv, 0, 1)

        def step(acc, kvt):
            acc = decay * acc + kvt
            return (acc, acc)
        _, accs = jax.lax.scan(step, jnp.zeros((b, H, HD), x.dtype), kv_t)
        wkv = jnp.swapaxes(accs, 0, 1) + u * kv
        rw = r * wkv
        mean = jnp.mean(rw, axis=-1, keepdims=True)
        var = jnp.var(rw, axis=-1, keepdims=True)
        ln = (rw - mean) * jax.lax.rsqrt(var + EPS)
        out = (jax.nn.sigmoid(g) * ln).reshape(b, n, d)
        return out @ Wo_w.T + Wo_b

    def _L0_ffn_ref(x, Wqkv, q_scale, k_scale, Wo, ln_g, ln_b, W1, b1, W2, b2):
        import jax, jax.numpy as jnp
        import numpy as np
        DIM = 128
        DEPTH = 6
        HEADS = 16
        DIM_HEAD = 64
        WINDOW = 32
        INNER = HEADS * DIM_HEAD
        DIM_INNER = int(DIM * 4 * 2 / 3)
        QK_SCALE = 8.0

        def shift_tokens(t):
            a, s = jnp.split(t, 2, -1)
            s = jnp.pad(s, ((0, 0), (1, 0), (0, 0)))[:, :-1]
            return jnp.concatenate([a, s], -1)

        def l2norm(t):
            return t / jnp.maximum(jnp.linalg.norm(t, axis=-1, keepdims=True), 1e-12)

        def rotate_half(x):
            x1, x2 = jnp.split(x, 2, -1)
            return jnp.concatenate([-x2, x1], -1)

        def rotary_tables(n):
            half = jnp.arange(0, DIM_HEAD, 2, dtype=jnp.float32)
            inv_freq = 1.0 / 10000.0 ** (half / DIM_HEAD)
            t = jnp.arange(n, dtype=jnp.float32)
            freqs = t[:, None] * inv_freq[None, :]
            freqs = jnp.concatenate([freqs, freqs], -1)
            base_scale = (half + 0.4 * DIM_HEAD) / (1.4 * DIM_HEAD)
            power = (t - n // 2) / (WINDOW // 2)
            scale = base_scale[None, :] ** power[:, None]
            scale = jnp.concatenate([scale, scale], -1)
            return (freqs, scale)

        def local_attention(q, k, v):
            b, h, n, d = q.shape
            w = WINDOW
            nw = n // w
            bq = q.reshape(b, h, nw, w, d)
            bk = k.reshape(b, h, nw, w, d)
            bv = v.reshape(b, h, nw, w, d)

            def look(t):
                p = jnp.pad(t, ((0, 0), (0, 0), (1, 0), (0, 0), (0, 0)))
                return jnp.concatenate([p[:, :, :nw], p[:, :, 1:]], axis=3)
            bk2, bv2 = (look(bk), look(bv))
            seq = jnp.arange(n).reshape(nw, w)
            seq_p = jnp.pad(seq, ((1, 0), (0, 0)), constant_values=-1)
            jt = jnp.concatenate([seq_p[:nw], seq_p[1:]], axis=1)
            it = seq[:, :, None]
            jb = jt[:, None, :]
            mask = (it < jb) | (it > jb + w) | (jb == -1)
            sim = jnp.einsum('bhwie,bhwje->bhwij', bq, bk2) * QK_SCALE
            sim = jnp.where(mask, -jnp.finfo(sim.dtype).max, sim)
            attn = jax.nn.softmax(sim, -1)
            out = jnp.einsum('bhwij,bhwje->bhwie', attn, bv2)
            return out.reshape(b, h, n, d)

        def attn_layer(x, Wqkv, qs, ksc, Wo):
            b, n, _ = x.shape
            qkv = x @ Wqkv
            q, k, v = jnp.split(qkv, 3, -1)
            sh = lambda t: t.reshape(b, n, HEADS, DIM_HEAD).transpose(0, 2, 1, 3)
            q, k, v = (sh(q), sh(k), sh(v))
            q = l2norm(q) * qs
            k = l2norm(k) * ksc
            freqs, scale = rotary_tables(n)
            cos, sin = (jnp.cos(freqs), jnp.sin(freqs))
            q = q * cos * scale + rotate_half(q) * sin * scale
            inv = 1.0 / scale
            k = k * cos * inv + rotate_half(k) * sin * inv
            out = local_attention(q, k, v)
            out = out.transpose(0, 2, 1, 3).reshape(b, n, INNER)
            return out @ Wo

        def ffn_layer(x, g, bln, W1, b1, W2, b2):
            mu = x.mean(-1, keepdims=True)
            var = ((x - mu) ** 2).mean(-1, keepdims=True)
            xn = (x - mu) / jnp.sqrt(var + 1e-05) * g + bln
            hg = xn @ W1 + b1
            a, gate = jnp.split(hg, 2, -1)
            return a * jax.nn.gelu(gate, approximate=False) @ W2 + b2
        for i in range(DEPTH):
            x = attn_layer(shift_tokens(x), Wqkv[i], q_scale[i], k_scale[i], Wo[i]) + x
            x = ffn_layer(shift_tokens(x), ln_g[i], ln_b[i], W1[i], b1[i], W2[i], b2[i]) + x
        return x

    def _L1_attn_ref(x, w_qkv, w_out, rel_bias):
        import jax, jax.numpy as jnp
        import numpy as np
        HEADS = 16
        DIM_HEAD = 64
        b, t, _ = x.shape
        h, dh = (HEADS, DIM_HEAD)
        scale = dh ** (-0.5)
        qkv = x @ w_qkv.T
        qkv = qkv.reshape(b, t, dh, 3, h).transpose(3, 0, 4, 1, 2)
        q, k, v = (qkv[0], qkv[1], qkv[2])
        scores = jnp.einsum('bhid,bhjd->bhij', q, k) * scale
        rel = jnp.arange(t)[None, :] - jnp.arange(t)[:, None] + (t - 1)
        bias = rel_bias[rel]
        scores = scores + bias.transpose(2, 0, 1)[None]
        attn = jax.nn.softmax(scores, axis=-1)
        out = jnp.einsum('bhij,bhjd->bhid', attn, v)
        out = out.transpose(0, 2, 1, 3).reshape(b, t, h * dh)
        return out @ w_out.T

    def _L1_ffn_ref(x, gate_w, w1, b1, w2, b2):
        import jax, jax.numpy as jnp
        import numpy as np
        TOP_K = 2
        B, S, D = x.shape
        E = gate_w.shape[1]
        xf = x.reshape(-1, D)
        router_logits = xf @ gate_w
        top_vals, top_idx = jax.lax.top_k(router_logits, TOP_K)
        top_w = jax.nn.softmax(top_vals, axis=-1)
        onehot = jax.nn.one_hot(top_idx, E, dtype=xf.dtype)
        cw = jnp.einsum('tk,tke->te', top_w, onehot)
        out = jnp.zeros_like(xf)
        for e in range(E):
            h = jax.nn.gelu(xf @ w1[e] + b1[e], approximate=False)
            out = out + cw[:, e:e + 1] * (h @ w2[e] + b2[e])
        return out.reshape(B, S, D)
    x = L0_attn_x
    mod = (_silu(L0_c) @ L0_wmod).reshape(L0_c.shape[0], 6, 1, -1)
    sa, ca, ga, sb, cb, gb = (mod[:, 0], mod[:, 1], mod[:, 2], mod[:, 3], mod[:, 4], mod[:, 5])
    ga = (2 * (ga >= 0) - 1) * jnp.maximum(jnp.abs(ga), 0.25)
    gb = (2 * (gb >= 0) - 1) * jnp.maximum(jnp.abs(gb), 0.25)
    h = _layernorm(x, axis=-1) * (1 + ca) + sa
    x = x + ga * _L0_attn_ref(h, L0_attn_Wg_w, L0_attn_Wg_b, L0_attn_Wr_w, L0_attn_Wr_b, L0_attn_Wk_w, L0_attn_Wk_b, L0_attn_Wv_w, L0_attn_Wv_b, L0_attn_Wo_w, L0_attn_Wo_b, L0_attn_mg, L0_attn_mr, L0_attn_mk, L0_attn_mv, L0_attn_w, L0_attn_u)
    h = _layernorm(x, axis=-1) * (1 + cb) + sb
    x = x + gb * _L0_ffn_ref(h, L0_ffn_Wqkv, L0_ffn_q_scale, L0_ffn_k_scale, L0_ffn_Wo, L0_ffn_ln_g, L0_ffn_ln_b, L0_ffn_W1, L0_ffn_b1, L0_ffn_W2, L0_ffn_b2)
    mod = (_silu(L1_c) @ L1_wmod).reshape(L1_c.shape[0], 6, 1, -1)
    sa, ca, ga, sb, cb, gb = (mod[:, 0], mod[:, 1], mod[:, 2], mod[:, 3], mod[:, 4], mod[:, 5])
    ga = (2 * (ga >= 0) - 1) * jnp.maximum(jnp.abs(ga), 0.25)
    gb = (2 * (gb >= 0) - 1) * jnp.maximum(jnp.abs(gb), 0.25)
    h = _layernorm(x, axis=-1) * (1 + ca) + sa
    x = x + ga * _L1_attn_ref(h, L1_attn_w_qkv, L1_attn_w_out, L1_attn_rel_bias)
    h = _layernorm(x, axis=-1) * (1 + cb) + sb
    x = x + gb * _L1_ffn_ref(h, L1_ffn_gate_w, L1_ffn_w1, L1_ffn_b1, L1_ffn_w2, L1_ffn_b2)
    return x

_drawn_inputs = setup_inputs


def setup_inputs(seed=0):
    import zlib

    import numpy as np

    out = dict(_drawn_inputs(seed))
    spreads = {'L0_attn_Wg_b': (0.0, 0.8),
     'L0_attn_Wr_b': (0.0, 0.278),
     'L0_attn_Wk_b': (0.0, 0.1),
     'L0_attn_Wv_b': (0.0, 0.271),
     'L0_attn_Wo_b': (0.0, 0.1),
     'L0_ffn_q_scale': (1.0, 0.6),
     'L0_ffn_k_scale': (1.0, 0.6),
     'L0_ffn_ln_g': (1.0, 0.6),
     'L0_ffn_ln_b': (0.0, 0.8),
     'L0_ffn_b1': (0.0, 0.8),
     'L0_ffn_b2': (0.0, 0.307),
     'L1_ffn_b1': (0.0, 2.0),
     'L1_ffn_b2': (0.0, 1.859)}
    factors = {'L0_ffn_W1': 5.471, 'L0_ffn_W2': 5.542, 'L1_attn_rel_bias': 64.0}
    for name, (base, spread) in spreads.items():
        noise = np.random.default_rng([zlib.crc32(name.encode()), seed]).standard_normal(out[name].shape)
        drawn = base * np.exp(spread * noise) if base else spread * noise
        out[name] = jnp.asarray(drawn.astype(out[name].dtype))
    for name, factor in factors.items():
        out[name] = (out[name] * factor).astype(out[name].dtype)
    return out
```

```python
from contextlib import ExitStack

import concourse.bass as bass
import concourse.mybir as mybir

F32 = mybir.dt.float32
BF16 = mybir.dt.bfloat16
U32 = mybir.dt.uint32
ALU = mybir.AluOpType
ACT = mybir.ActivationFunctionType
AX = mybir.AxisListType

P = 128
B = 2
N = 1024
TOK = B * N
CH = 512
NCH = TOK // CH
PAD = 33

LAYERS = 6
HEADS = 16
HD = 64
PAIRS = HEADS // 2
WIN = 32
BLK = 128
WPB = BLK // WIN
SLOTS = TOK // BLK
INNER = HEADS * HD
FF = 341
FB = 3
FROWS = [128, 128, FF - 256]

EXPERTS = 8
EF = 512
EFB = EF // P
TB = TOK // P
LN_EPS = 1e-5


def build(nc, A, out):
    with ExitStack() as whole:
        def sb(name, shape, dt=F32, ctx=whole):
            return ctx.enter_context(nc.sbuf_tensor(name, shape, dt))

        def sem(name, ctx=whole):
            return ctx.enter_context(nc.semaphore(name))

        bank = whole.enter_context(nc.psum_tensor("bank", [P, 8, CH], F32))

        x_main = sb("x_main", [P, B, N])
        h_in = sb("h_in", [P, B, PAD + N])
        h_mid = sb("h_mid", [P, B, PAD + N])
        ident = sb("ident", [P, P])
        mean_w = sb("mean_w", [P, P])
        eps = sb("eps", [P, 1])
        mod = sb("mod", [P, 2, 6, B])
        gate_a = sb("gate_a", [P, 2, 2, B])

        def x_chunk(c):
            return x_main[:, c // 2, (c % 2) * CH:(c % 2 + 1) * CH]

        def padded(t, c):
            return t[:, c // 2, PAD + (c % 2) * CH:PAD + (c % 2 + 1) * CH]

        with ExitStack() as ctx:
            wmod = sb("wmod", [P, 2, 6 * P], ctx=ctx)
            c_t = sb("c_t", [P, 2, B], ctx=ctx)
            c_silu = sb("c_silu", [P, 2, B], ctx=ctx)
            s_in = sem("s_in")
            s_const = sem("s_const")
            s_silu = sem("s_silu")
            s_mod_mm = sem("s_mod_mm")
            s_mod = sem("s_mod")
            block = ctx.enter_context(nc.Block())

            @block.sync
            def _(sp):
                sp.dma_start(c_t[:, :, :], A["c_t"]).then_inc(s_in, 16)
                sp.dma_start(wmod[:, :, :], A["wmod"]).then_inc(s_in, 16)
                sp.dma_start(x_main[:, :, :], A["x_t"]).then_inc(s_in, 16)
                sp.dma_start(ident[:, :], A["ident"]).then_inc(s_in, 16)
                sp.wait_ge(s_in, 64)

            @block.gpsimd
            def _(pool):
                pool.memset(mean_w[:, :], 1.0 / P).then_inc(s_const, 1)
                pool.memset(eps[:, :], LN_EPS).then_inc(s_const, 1)
                pool.memset(h_in[:, :, 0:PAD], 0.0).then_inc(s_const, 1)
                pool.memset(h_mid[:, :, 0:PAD], 0.0).then_inc(s_const, 1)
                pool.wait_ge(s_const, 4)

            @block.scalar
            def _(act):
                act.wait_ge(s_in, 64)
                act.activation(c_silu[:, :, :], c_t[:, :, :], ACT.Silu).then_inc(s_silu, 1)

            @block.tensor
            def _(pe):
                pe.wait_ge(s_silu, 1)
                for la in range(2):
                    for j in range(6):
                        mm = pe.matmul(bank[:, 0, (la * 6 + j) * B:(la * 6 + j + 1) * B],
                                       wmod[:, la, j * P:(j + 1) * P], c_silu[:, la, :], start=True, stop=True)
                mm.then_inc(s_mod_mm, 1)

            @block.vector
            def _(dve):
                flat = mod[:, :, :, :].rearrange("p l j b -> p (l j b)")
                dve.wait_ge(s_mod_mm, 1)
                dve.tensor_copy(flat, bank[:, 0, 0:24]).then_inc(s_mod, 1)
                dve.wait_ge(s_mod, 1)
                n = 1
                for la in range(2):
                    for i, j in enumerate((2, 5)):
                        g = mod[:, la, j, :]
                        a = gate_a[:, la, i, :]
                        dve.tensor_scalar(a, g, 0.0, 2.0, ALU.is_ge, ALU.mult).then_inc(s_mod, 1)
                        dve.wait_ge(s_mod, n + 1)
                        dve.tensor_scalar(a, a, -1.0, None, ALU.add).then_inc(s_mod, 1)
                        dve.wait_ge(s_mod, n + 2)
                        dve.tensor_tensor(g, g, a, ALU.mult).then_inc(s_mod, 1)
                        dve.wait_ge(s_mod, n + 3)
                        dve.scalar_tensor_tensor(out=g, in0=g, scalar=0.25, in1=a, op0=ALU.max, op1=ALU.mult)\
                           .then_inc(s_mod, 1)
                        dve.wait_ge(s_mod, n + 4)
                        dve.tensor_scalar(mod[:, la, j - 1, :], mod[:, la, j - 1, :], 1.0, None,
                                          ALU.add).then_inc(s_mod, 1)
                        dve.wait_ge(s_mod, n + 5)
                        n += 5

        def layer_norm(tag, ctx, work, src, dst, scale, shift, mean_bank, var_bank, var_free=None):
            centered, squares, dev = work
            s_mean = sem(f"s_{tag}_mean", ctx)
            s_cen = sem(f"s_{tag}_centered", ctx)
            s_sq = sem(f"s_{tag}_squares", ctx)
            s_var = sem(f"s_{tag}_var", ctx)
            s_dev = sem(f"s_{tag}_dev", ctx)
            s_rec = sem(f"s_{tag}_recip", ctx)
            s_nrm = sem(f"s_{tag}_scaled", ctx)
            s_out = sem(f"s_{tag}_out", ctx)

            def pe_mean(pe, c):
                if c >= 2:
                    pe.wait_ge(s_cen, c - 1)
                pe.matmul(bank[:, mean_bank(c), :], mean_w[:, :], src(c), start=True, stop=True).then_inc(s_mean, 1)

            def dve_center(dve, c):
                dve.wait_ge(s_mean, c + 1)
                if c >= 2:
                    dve.wait_ge(s_out, c - 1)
                dve.tensor_tensor(centered(c), src(c), bank[:, mean_bank(c), :], ALU.subtract).then_inc(s_cen, 1)

            def act_square(act, c):
                act.wait_ge(s_cen, c + 1)
                if c >= 2:
                    act.wait_ge(s_var, c - 1)
                act.activation(squares(c), centered(c), ACT.Square).then_inc(s_sq, 1)

            def pe_var(pe, c):
                pe.wait_ge(s_sq, c + 1)
                if c >= 2:
                    pe.wait_ge(s_dev, c - 1)
                    if var_free is not None:
                        var_free(pe, c)
                pe.matmul(bank[:, var_bank(c), :], mean_w[:, :], squares(c), start=True, stop=True).then_inc(s_var, 1)

            def act_dev(act, c):
                act.wait_ge(s_var, c + 1)
                if c >= 2:
                    act.wait_ge(s_nrm, c - 1)
                act.activation(dev(c), bank[:, var_bank(c), :], ACT.Sqrt, bias=eps[:, :]).then_inc(s_dev, 1)

            def dve_norm(dve, c):
                dve.wait_ge(s_dev, c + 1)
                dve.reciprocal(dev(c), dev(c)).then_inc(s_rec, 1)
                dve.wait_ge(s_rec, c + 1)
                dve.tensor_tensor(centered(c), centered(c), dev(c), ALU.mult).then_inc(s_nrm, 1)
                dve.wait_ge(s_nrm, c + 1)
                dve.tensor_scalar(dst(c), centered(c), scale(c), shift(c), ALU.mult, ALU.add).then_inc(s_out, 1)

            return pe_mean, dve_center, act_square, pe_var, act_dev, dve_norm, s_out

        def modulated_norm(tag, la, first, dst):
            with ExitStack() as ctx:
                w = sb(f"{tag}_work", [P, 6, CH], ctx=ctx)
                steps = layer_norm(
                    tag, ctx, [lambda c, o=o: w[:, o + c % 2, :] for o in (0, 2, 4)], x_chunk, dst,
                    lambda c: mod[:, la, first + 1, c // 2:c // 2 + 1], lambda c: mod[:, la, first, c // 2:c // 2 + 1],
                    lambda c: c % 2, lambda c: 2 + c % 2)
                pe_mean, dve_center, act_square, pe_var, act_dev, dve_norm, s_out = steps
                block = ctx.enter_context(nc.Block(no_gpsimd_drain=True))

                @block.tensor
                def _(pe):
                    pe_mean(pe, 0)
                    for c in range(NCH):
                        if c + 1 < NCH:
                            pe_mean(pe, c + 1)
                        pe_var(pe, c)

                @block.scalar
                def _(act):
                    for c in range(NCH):
                        act_square(act, c)
                        act_dev(act, c)

                @block.vector
                def _(dve):
                    dve_center(dve, 0)
                    for c in range(NCH):
                        if c + 1 < NCH:
                            dve_center(dve, c + 1)
                        dve_norm(dve, c)
                    dve.wait_ge(s_out, NCH)

        time_mixing(nc, A, sb, sem, bank, x_main, x_chunk, eps, mod, modulated_norm, h_mid)
        modulated_norm("ln_l0b", 0, 3, lambda c: padded(h_in, c))
        local_transformer(nc, A, sb, sem, bank, ident, h_in, h_mid, padded, layer_norm)
        add_gated(nc, sb, sem, x_chunk, mod, 0, lambda c: padded(h_in, c))
        modulated_norm("ln_l1a", 1, 0, lambda c: padded(h_in, c))
        full_attention(nc, A, sb, sem, bank, ident, h_in, padded, x_chunk, mod)
        modulated_norm("ln_l1b", 1, 3, lambda c: padded(h_in, c))
        experts(nc, A, sb, sem, bank, ident, h_in, x_main, mod, out)


def time_mixing(nc, A, sb, sem, bank, x_main, x_chunk, eps, mod, modulated_norm, h_mid):
    with ExitStack() as ctx:
        h = sb("tm_h", [P, B, 1 + N], ctx=ctx)
        modulated_norm("ln_l0a", 0, 0, lambda c: h[:, c // 2, 1 + (c % 2) * CH:1 + (c % 2 + 1) * CH])
        w = sb("tm_w", [P, 5, P], ctx=ctx)
        vec = sb("tm_vec", [P, 11], ctx=ctx)
        group_mean = sb("tm_group_mean", [P, P], ctx=ctx)
        diff = sb("tm_diff", [P, 2, CH], ctx=ctx)
        mix = sb("tm_mix", [P, 2, 4, CH], ctx=ctx)
        gate = sb("tm_gate", [P, B, N], ctx=ctx)
        recv = sb("tm_recv", [P, B, N], ctx=ctx)
        key = sb("tm_key", [P, 2, CH], ctx=ctx)
        kv = sb("tm_kv", [P, B, N], ctx=ctx)
        acc = sb("tm_acc", [P, B, N], ctx=ctx)
        decay = sb("tm_decay", [P, 2], ctx=ctx)
        s_w = sem("s_tm_weights")
        s_wrap = sem("s_tm_wrap")
        s_diff = sem("s_tm_diff")
        s_mix = sem("s_tm_mix")
        s_proj = sem("s_tm_proj")
        s_gate = sem("s_tm_gate")
        s_key = sem("s_tm_key")
        s_recv = sem("s_tm_recv")
        s_kv = sem("s_tm_kv")
        s_decay = sem("s_tm_decay")

        def at(t, c):
            return t[:, c // 2, (c % 2) * CH:(c % 2 + 1) * CH]

        def shifted(c):
            return h[:, c // 2, (c % 2) * CH:(c % 2 + 1) * CH]

        def straight(c):
            return h[:, c // 2, 1 + (c % 2) * CH:1 + (c % 2 + 1) * CH]

        with nc.Block(no_gpsimd_drain=True) as block:
            @block.sync
            def _(sp):
                sp.dma_start(w[:, :, :], A["tm_w"]).then_inc(s_w, 16)
                sp.dma_start(vec[:, :], A["tm_vec"]).then_inc(s_w, 16)
                sp.dma_start(group_mean[:, :], A["group_mean"]).then_inc(s_w, 16)
                sp.wait_ge(s_w, 48)

            @block.scalar
            def _(act):
                act.copy(h[:, :, 0:1], h[:, :, N:N + 1]).then_inc(s_wrap, 1)
                act.wait_ge(s_w, 48)
                act.activation(decay[:, 0:1], vec[:, 9:10], ACT.Exp).then_inc(s_decay, 1)
                act.wait_ge(s_decay, 1)
                act.activation(decay[:, 1:2], decay[:, 0:1], ACT.Exp, scale=-1.0).then_inc(s_decay, 1)
                act.wait_ge(s_decay, 2)
                for c in range(NCH):
                    q = 4 * (c % 2)
                    act.wait_ge(s_proj, 4 * c + 3)
                    if c >= 2:
                        act.wait_ge(s_kv, c - 1)
                    act.activation(key[:, c % 2, :], bank[:, q + 2, :], ACT.Identity, bias=vec[:, 2:3]).then_inc(s_key, 1)
                    act.activation(at(recv, c), bank[:, q + 1, :], ACT.Identity, bias=vec[:, 1:2]).then_inc(s_recv, 1)
                    act.activation(at(gate, c), bank[:, q, :], ACT.Sigmoid, bias=vec[:, 0:1]).then_inc(s_gate, 1)
                act.wait_ge(s_gate, NCH)
                act.wait_ge(s_recv, NCH)

            @block.vector
            def _(dve):
                dve.wait_ge(s_w, 48)
                dve.wait_ge(s_wrap, 1)
                for c in range(NCH):
                    if c >= 2:
                        dve.wait_ge(s_mix, 4 * (c - 1))
                    dve.tensor_tensor(diff[:, c % 2, :], straight(c), shifted(c), ALU.subtract).then_inc(s_diff, 1)
                    dve.wait_ge(s_diff, c + 1)
                    if c >= 2:
                        dve.wait_ge(s_proj, 4 * (c - 1))
                    for i in range(4):
                        dve.scalar_tensor_tensor(out=mix[:, c % 2, i, :], in0=diff[:, c % 2, :],
                                                 scalar=vec[:, 5 + i:6 + i], in1=shifted(c),
                                                 op0=ALU.mult, op1=ALU.add).then_inc(s_mix, 1)
                    dve.wait_ge(s_key, c + 1)
                    dve.wait_ge(s_proj, 4 * c + 4)
                    dve.scalar_tensor_tensor(out=at(kv, c), in0=bank[:, 4 * (c % 2) + 3, :], scalar=vec[:, 3:4],
                                             in1=key[:, c % 2, :], op0=ALU.add, op1=ALU.mult).then_inc(s_kv, 1)
                dve.wait_ge(s_kv, NCH)

            @block.tensor
            def _(pe):
                pe.wait_ge(s_w, 48)
                for c in range(NCH):
                    if c >= 2:
                        pe.wait_ge(s_gate, c - 1)
                        pe.wait_ge(s_kv, c - 1)
                    for i in range(4):
                        pe.wait_ge(s_mix, 4 * c + i + 1)
                        pe.matmul(bank[:, 4 * (c % 2) + i, :], w[:, i, :], mix[:, c % 2, i, :],
                                  start=True, stop=True).then_inc(s_proj, 1)

        s_scan = sem("s_tm_scan")
        s_wkv = sem("s_tm_wkv")
        s_rw = sem("s_tm_rw")
        s_mean = sem("s_tm_gmean")
        s_cen = sem("s_tm_gcentered")
        s_sq = sem("s_tm_gsquares")
        s_var = sem("s_tm_gvar")
        s_dev = sem("s_tm_gdev")
        s_rec = sem("s_tm_grecip")
        s_nrm = sem("s_tm_gnorm")
        s_gated = sem("s_tm_gated")
        s_o = sem("s_tm_o")
        s_og = sem("s_tm_ogated")
        s_x = sem("s_tm_x")
        sq, dev = mix[:, 0, :, :], mix[:, 1, :, :]
        og = diff
        with nc.Block(no_gpsimd_drain=True) as block:
            @block.vector
            def _(dve):
                for b in range(B):
                    dve.tensor_tensor_scan(acc[:, b, :], decay[:, 1:2].to_broadcast([P, N]), kv[:, b, :], 0.0,
                                           ALU.mult, ALU.add).then_inc(s_scan, 1)
                for c in range(NCH):
                    dve.wait_ge(s_scan, c // 2 + 1)
                    dve.scalar_tensor_tensor(out=at(acc, c), in0=at(kv, c), scalar=vec[:, 10:11], in1=at(acc, c),
                                             op0=ALU.mult, op1=ALU.add).then_inc(s_wkv, 1)
                    dve.wait_ge(s_wkv, c + 1)
                    dve.tensor_tensor(at(recv, c), at(recv, c), at(acc, c), ALU.mult).then_inc(s_rw, 1)
                for c in range(NCH):
                    dve.wait_ge(s_mean, c + 1)
                    dve.tensor_tensor(at(recv, c), at(recv, c), bank[:, c, :], ALU.subtract).then_inc(s_cen, 1)
                for c in range(NCH):
                    dve.wait_ge(s_dev, c + 1)
                    dve.reciprocal(dev[:, c, :], dev[:, c, :]).then_inc(s_rec, 1)
                    dve.wait_ge(s_rec, c + 1)
                    dve.tensor_tensor(at(recv, c), at(recv, c), dev[:, c, :], ALU.mult).then_inc(s_nrm, 1)
                    dve.wait_ge(s_nrm, c + 1)
                    dve.tensor_tensor(at(recv, c), at(recv, c), at(gate, c), ALU.mult).then_inc(s_gated, 1)
                for c in range(NCH):
                    dve.wait_ge(s_o, c + 1)
                    if c >= 2:
                        dve.wait_ge(s_x, c - 1)
                    dve.tensor_scalar(og[:, c % 2, :], bank[:, c, :], vec[:, 4:5], mod[:, 0, 2, c // 2:c // 2 + 1],
                                      ALU.add, ALU.mult).then_inc(s_og, 1)
                    dve.wait_ge(s_og, c + 1)
                    dve.tensor_tensor(x_chunk(c), x_chunk(c), og[:, c % 2, :], ALU.add).then_inc(s_x, 1)
                dve.wait_ge(s_x, NCH)

            @block.scalar
            def _(act):
                for c in range(NCH):
                    act.wait_ge(s_cen, c + 1)
                    act.activation(sq[:, c, :], at(recv, c), ACT.Square).then_inc(s_sq, 1)
                for c in range(NCH):
                    act.wait_ge(s_var, c + 1)
                    act.activation(dev[:, c, :], bank[:, 4 + c, :], ACT.Sqrt, bias=eps[:, :]).then_inc(s_dev, 1)

            @block.tensor
            def _(pe):
                for c in range(NCH):
                    pe.wait_ge(s_rw, c + 1)
                    pe.matmul(bank[:, c, :], group_mean[:, :], at(recv, c), start=True, stop=True).then_inc(s_mean, 1)
                for c in range(NCH):
                    pe.wait_ge(s_sq, c + 1)
                    pe.matmul(bank[:, 4 + c, :], group_mean[:, :], sq[:, c, :], start=True, stop=True).then_inc(s_var, 1)
                for c in range(NCH):
                    pe.wait_ge(s_gated, c + 1)
                    pe.matmul(bank[:, c, :], w[:, 4, :], at(recv, c), start=True, stop=True).then_inc(s_o, 1)


def add_gated(nc, sb, sem, x_chunk, mod, la, src):
    s_x = sem(f"s_gated{la}")
    with nc.Block(no_gpsimd_drain=True) as block:
        @block.vector
        def _(dve):
            for c in range(NCH):
                dve.scalar_tensor_tensor(out=x_chunk(c), in0=src(c), scalar=mod[:, la, 5, c // 2:c // 2 + 1],
                                         in1=x_chunk(c), op0=ALU.mult, op1=ALU.add).then_inc(s_x, 1)
            dve.wait_ge(s_x, NCH)


def local_transformer(nc, A, sb, sem, bank, ident, h_in, h_mid, padded, layer_norm):
    with ExitStack() as ctx:
        def buf(name, shape, dt=F32):
            return sb(f"lt_{name}", shape, dt, ctx=ctx)

        w_qkv = buf("w_qkv", [P, 3 * INNER])
        w_o = buf("w_o", [P, PAIRS, P])
        w_1 = buf("w_1", [P, 2 * FF])
        w_2 = buf("w_2", [P, FB, P])
        lvec = buf("lvec", [P, 9])
        qk_scale = buf("qk_scale", [P, 2, HD])
        cos_raw = buf("cos_raw", [P, SLOTS // 2, 2 * HD])
        sin_raw = buf("sin_raw", [P, SLOTS // 2, 2 * HD])
        cos = buf("cos", [P, SLOTS // 2, 2 * HD])
        sin = buf("sin", [P, SLOTS // 2, 2 * HD])
        mask_f = buf("mask_f", [P, 2, HD])
        mask = buf("mask", [P, 2, PAIRS * HD], BF16)
        ident_b = buf("ident_b", [P, P], BF16)
        x_s = buf("x_s", [P, 2, WIN + BLK])
        qk = buf("qk", [P, 2, 2 * INNER])
        sq = buf("sq", [P, 2 * INNER])
        ssq = buf("ssq", [P, 2, 2 * HEADS])
        rn = buf("rn", [P, 2, 2 * HEADS])
        qn = buf("qn", [P, 2 * INNER])
        t_cos = buf("t_cos", [P, 2 * INNER])
        t_sin = buf("t_sin", [P, 2 * INNER])
        qr = buf("qr", [P, 2, 2 * INNER])
        q_t = buf("q_t", [P, 2, PAIRS, BLK])
        k_t = buf("k_t", [P, 2, PAIRS, WIN + BLK])
        v = buf("v", [P, 2, WPB, PAIRS, HD])
        row_max = buf("row_max", [P, 2, PAIRS])
        prob = buf("prob", [P, 2, PAIRS, 2, HD])
        row_sum = buf("row_sum", [P, 2, HEADS])
        prob_t = buf("prob_t", [P, 2, PAIRS, BLK])
        att = buf("att", [P, 2, PAIRS, 2, HD])
        att_t = buf("att_t", [P, 2, PAIRS, BLK])
        xs2, fx = sq[:, 0:1024].rearrange("p (r n) -> p r n", r=2), \
            sq[:, 1024:2048].rearrange("p (r n) -> p r n", r=2)
        fsq = t_cos[:, 0:1024].rearrange("p (r n) -> p r n", r=2)
        fdev = t_cos[:, 1024:2048].rearrange("p (r n) -> p r n", r=2)
        fxn = qn[:, 0:1024].rearrange("p (r n) -> p r n", r=2)
        fgate = qn[:, 1024:2048].rearrange("p (r n) -> p r n", r=2)
        fh = qr[:, :, :].rearrange("p r (j n) -> p r j n", j=4)

        PJ = (0, 1)
        SC = (2, 3)
        AV = (4, 5)
        MISC = (6, 7)

        s_tab = sem("s_lt_tables")
        s_cast = sem("s_lt_cast")
        s_w0 = sem("s_lt_first_weights")
        with nc.Block() as block:
            @block.sync
            def _(sp):
                sp.dma_start(cos_raw[:, :, :], A["cos"]).then_inc(s_tab, 16)
                sp.dma_start(sin_raw[:, :, :], A["sin"]).then_inc(s_tab, 16)
                sp.dma_start(mask_f[:, :, :], A["mask"]).then_inc(s_tab, 16)
                sp.dma_start(w_qkv[:, :], A["lt_wqkv"][0]).then_inc(s_w0, 16)
                sp.dma_start(qk_scale[:, :, :].rearrange("p a d -> p (a d)"),
                             A["lt_qkscale"][0].to_broadcast([P, 2 * HD])).then_inc(s_w0, 16)
                sp.wait_ge(s_tab, 48)
                sp.wait_ge(s_w0, 32)

            @block.vector
            def _(dve):
                dve.wait_ge(s_tab, 48)
                for i in range(2):
                    dve.tensor_copy(mask[:, i, :].rearrange("p (a k) -> p a k", a=PAIRS),
                                    mask_f[:, i:i + 1, :].to_broadcast([P, PAIRS, HD])).then_inc(s_cast, 1)
                dve.tensor_copy(ident_b[:, :], ident[:, :]).then_inc(s_cast, 1)
                dve.wait_ge(s_cast, 3)

        names = ("weights next cleared scales staged proj proj_out squared sumsq norm clamped inv_norm normed rot_cos rot_sin "
                 "rotated lookback misc misc_out scores rowmax shifted probs rowsum inv_sum av av_out "
                 "xs2 gate_mm value_mm gated hidden down ff_out").split()
        first = {n: sem(f"s_lt_{n}", ctx) for n in names}
        S = type("S", (), first)
        norm_steps = layer_norm(
            "lt_norm", ctx, [lambda c: fx[:, c % 2, :], lambda c: fsq[:, c % 2, :], lambda c: fdev[:, c % 2, :]],
            lambda c: xs2[:, c % 2, :], lambda c: fxn[:, c % 2, :], lambda c: lvec[:, 0:1], lambda c: lvec[:, 1:2],
            lambda c: SC[c % 2], lambda c: AV[c % 2], lambda pe, c: pe.wait_ge(S.ff_out, c - 1))
        pe_mean, dve_center, act_square, pe_var, act_dev, dve_norm, s_normed = norm_steps
        numbers = [s.num for s in first.values()] + [s_normed.num]
        span = range(min(numbers), max(numbers) + 1)

        turn = {}
        for s in range(-1, SLOTS + 2):
            for kind, of, groups in (("turn", s, 4), ("att", s - 2, 2), ("prob", s - 1, 2), ("out", s - 2, 1)):
                if 0 <= of < SLOTS:
                    for g in range(groups):
                        turn[kind, of, g] = len(turn)

        def misc(kind, s, g):
            return MISC[turn[kind, s, g] % 2]

        def live(s):
            return 0 <= s < SLOTS

        def tokens(t, s):
            lo = PAD + (s // 2) * BLK
            return t[:, s % 2, lo:lo + BLK]

        with nc.Fori(0, LAYERS) as layer:
            with nc.Block(no_gpsimd_drain=True) as block:
                @block.sync
                def _(sp):
                    sp.dma_start(w_o[:, :, :], A["lt_wo"][layer]).then_inc(S.weights, 16)
                    sp.dma_start(w_1[:, :], A["lt_w1"][layer]).then_inc(S.weights, 16)
                    sp.dma_start(w_2[:, :, :], A["lt_w2"][layer]).then_inc(S.weights, 16)
                    sp.dma_start(lvec[:, :], A["lt_vec"][layer]).then_inc(S.weights, 16)
                    sp.wait_ge(S.scales, 3)
                    sp.dma_start(qk_scale[:, :, :].rearrange("p a d -> p (a d)"),
                                 A["lt_qkscale"][layer + 1].to_broadcast([P, 2 * HD])).then_inc(S.next, 16)
                    sp.wait_ge(S.proj, 8 * SLOTS)
                    sp.dma_start(w_qkv[:, :], A["lt_wqkv"][layer + 1]).then_inc(S.next, 16)
                    sp.wait_ge(S.next, 32)
                    sp.wait_ge(S.weights, 64)

                @block.gpsimd
                def _(pool):
                    pool.memset(k_t[:, :, :, 0:WIN], 0.0).then_inc(S.cleared, 1)
                    half = "p t (a i d) -> p (t a) i d"
                    pool.tensor_tensor(cos[:, :, :], cos_raw[:, :, :],
                                       qk_scale[:, :, :].rearrange("p a d -> p (a d)").unsqueeze(1).to_broadcast([P, SLOTS // 2, 2 * HD]),
                                       ALU.mult).then_inc(S.scales, 1)
                    for i in range(2):
                        o = slice(32 * i, 32 * i + 32)
                        r = slice(32 - 32 * i, 64 - 32 * i)
                        pool.tensor_tensor(
                            sin[:, :, :].rearrange("p t (a d) -> p t a d", a=2)[:, :, :, o],
                            sin_raw[:, :, :].rearrange("p t (a d) -> p t a d", a=2)[:, :, :, o],
                            qk_scale[:, :, r].unsqueeze(1).to_broadcast([P, SLOTS // 2, 2, 32]),
                            ALU.mult).then_inc(S.scales, 1)
                    pool.wait_ge(S.scales, 3)
                    for s in range(-1, SLOTS + 2):
                        n = s + 1
                        if live(n):
                            pool.wait_ge(S.normed, n + 1)
                            if n >= 1:
                                pool.wait_ge(S.rotated, n)
                            src = qn[:, :].rearrange("p (a h i d) -> p a h i d", a=2, h=HEADS, i=2)
                            dst = t_sin[:, :].rearrange("p (a h i d) -> p a h i d", a=2, h=HEADS, i=2)
                            tab = sin[:, n // 2, :].rearrange("p (a i d) -> p a i d", a=2, i=2)
                            for i in range(2):
                                pool.tensor_tensor(dst[:, :, :, i, :], src[:, :, :, 1 - i, :],
                                                   tab[:, :, i, :].unsqueeze(2).to_broadcast([P, 2, HEADS, 32]),
                                                   ALU.mult).then_inc(S.rot_sin, 1)
                            pool.wait_ge(S.rot_cos, n + 1)
                            pool.wait_ge(S.rot_sin, 2 * (n + 1))
                            if n >= 2:
                                pool.wait_ge(S.misc, turn["turn", n - 2, 3] + 1)
                            pool.tensor_tensor(qr[:, n % 2, :], t_cos[:, :], t_sin[:, :], ALU.add).then_inc(S.rotated, 1)

                @block.tensor
                def _(pe):
                    def free_misc(kind, s, g):
                        n = turn[kind, s, g]
                        if n >= 2:
                            pe.wait_ge(S.misc_out, n - 1)

                    def project_qk(s):
                        pe.wait_ge(S.staged, 2 * (s + 1))
                        for j in range(4):
                            u = 8 * s + j
                            if u >= 2:
                                pe.wait_ge(S.proj_out, u - 1)
                            pe.matmul(bank[:, PJ[u % 2], :], x_s[:, s % 2, WIN:WIN + BLK],
                                      w_qkv[:, j * CH:(j + 1) * CH], start=True, stop=True).then_inc(S.proj, 1)

                    def project_v(s):
                        heads = w_qkv[:, 2 * INNER:3 * INNER].rearrange("p (h a d) -> p h a d", a=2, d=HD)
                        for w in range(WPB):
                            u = 8 * s + 4 + w
                            pe.wait_ge(S.proj_out, u - 1)
                            for par in range(2):
                                mm = pe.matmul(bank[64 * par:64 * par + 64, PJ[u % 2], :].rearrange("p (h d) -> p h d", d=HD),
                                               x_s[:, s % 2, WIN * w:WIN * w + 2 * WIN], heads[:, :, par, :],
                                               start=True, stop=True)
                            mm.then_inc(S.proj, 1)

                    def turn_qk(s):
                        pe.wait_ge(S.rotated, s + 1)
                        for g in range(4):
                            free_misc("turn", s, g)
                            for i in range(4):
                                mm = pe.transpose(bank[:, misc("turn", s, g), i * P:(i + 1) * P],
                                                  qr[:, s % 2, (4 * g + i) * P:(4 * g + i + 1) * P], ident[:, :])
                            mm.then_inc(S.misc, 1)

                    def scores(s):
                        pe.wait_ge(S.misc_out, turn["turn", s, 3] + 1)
                        if s < 2:
                            pe.wait_ge(S.cleared, 1)
                        for par in range(2):
                            if s >= 1:
                                pe.wait_ge(S.shifted, 2 * s - 1 + par)
                            pe.matmul(bank[:, SC[par], :], ident_b[:, :], mask[:, 0 if s < 2 else 1, :],
                                      start=True, stop=False, skip_group_check=True)
                            f = slice(64 * par, 64 * par + 64)
                            for w in range(WPB):
                                for hp in range(PAIRS):
                                    mm = pe.matmul(bank[WIN * w:WIN * w + WIN, SC[par], hp * HD:(hp + 1) * HD],
                                                   q_t[f, s % 2, hp, WIN * w:WIN * w + WIN],
                                                   k_t[f, s % 2, hp, WIN * w:WIN * w + 2 * WIN],
                                                   start=False, stop=True, skip_group_check=True)
                            mm.then_inc(S.scores, 1)

                    def turn_prob(s):
                        pe.wait_ge(S.probs, s + 1)
                        for g in range(2):
                            free_misc("prob", s, g)
                            for i in range(4):
                                hp = 4 * g + i
                                mm = pe.transpose(bank[:, misc("prob", s, g), i * P:(i + 1) * P],
                                                  prob[:, s % 2, hp, :, :].rearrange("p a k -> p (a k)"), ident[:, :])
                            mm.then_inc(S.misc, 1)

                    def weigh_v(s):
                        pe.wait_ge(S.misc_out, turn["prob", s, 1] + 1)
                        pe.wait_ge(S.proj_out, 8 * (s + 1))
                        for par in range(2):
                            if s >= 1:
                                pe.wait_ge(S.av_out, 2 * s - 1 + par)
                            f = slice(64 * par, 64 * par + 64)
                            for w in range(WPB):
                                for hp in range(PAIRS):
                                    mm = pe.matmul(bank[WIN * w:WIN * w + WIN, AV[par], hp * HD:(hp + 1) * HD],
                                                   prob_t[f, s % 2, hp, WIN * w:WIN * w + WIN],
                                                   v[f, s % 2, w, hp, :], start=True, stop=True)
                            mm.then_inc(S.av, 1)

                    def turn_att(s):
                        pe.wait_ge(S.av_out, 2 * (s + 1))
                        for g in range(2):
                            free_misc("att", s, g)
                            for i in range(4):
                                mm = pe.transpose(bank[:, misc("att", s, g), i * P:(i + 1) * P],
                                                  att[:, s % 2, 4 * g + i, :, :].rearrange("p a d -> p (a d)"), ident[:, :])
                            mm.then_inc(S.misc, 1)

                    def project_out(s):
                        if s == 0:
                            pe.wait_ge(S.weights, 64)
                        free_misc("out", s, 0)
                        pe.wait_ge(S.misc_out, turn["att", s, 1] + 1)
                        o = bank[:, misc("out", s, 0), 0:BLK]
                        pe.matmul(o, ident[:, :], tokens(h_in, s), start=True, stop=False)
                        for hp in range(PAIRS):
                            mm = pe.matmul(o, w_o[:, hp, :], att_t[:, s % 2, hp, :], start=False, stop=hp == PAIRS - 1)
                        mm.then_inc(S.misc, 1)

                    for s in range(-1, SLOTS + 2):
                        if live(s + 1):
                            project_qk(s + 1)
                        if live(s):
                            turn_qk(s)
                        if live(s - 2):
                            turn_att(s - 2)
                        if live(s - 1):
                            turn_prob(s - 1)
                        if live(s):
                            scores(s)
                        if live(s - 2):
                            project_out(s - 2)
                        if live(s - 1):
                            weigh_v(s - 1)
                        if live(s + 1):
                            project_v(s + 1)

                    def up(c):
                        pe.wait_ge(s_normed, c + 1)
                        for j in range(FB):
                            n = FB * c + j
                            m = FROWS[j]
                            if n >= 2:
                                pe.wait_ge(S.gated, n - 1)
                                pe.wait_ge(S.hidden, n - 1)
                            pe.matmul(bank[0:m, PJ[n % 2], :], w_1[:, FF + j * P:FF + j * P + m], fxn[:, c % 2, :],
                                      start=True, stop=True).then_inc(S.gate_mm, 1)
                            pe.matmul(bank[0:m, MISC[n % 2], :], w_1[:, j * P:j * P + m], fxn[:, c % 2, :],
                                      start=True, stop=True).then_inc(S.value_mm, 1)

                    def down(c):
                        pe.wait_ge(S.hidden, FB * (c + 1))
                        for j in range(FB):
                            m = FROWS[j]
                            mm = pe.matmul(bank[:, AV[c % 2], :], w_2[0:m, j, :], fh[0:m, c % 2, j, :],
                                           start=j == 0, stop=j == FB - 1)
                        mm.then_inc(S.down, 1)

                    pe.wait_ge(S.xs2, 2)
                    pe_mean(pe, 0)
                    for c in range(NCH):
                        if c + 1 < NCH:
                            pe.wait_ge(S.xs2, 2 * (c + 2))
                            pe_mean(pe, c + 1)
                        pe_var(pe, c)
                        if c >= 1:
                            up(c - 1)
                            down(c - 1)
                    up(NCH - 1)
                    down(NCH - 1)

                @block.scalar
                def _(act):
                    def empty_qk(s):
                        if s >= 2:
                            act.wait_ge(S.normed, s - 1)
                        for j in range(4):
                            act.wait_ge(S.proj, 8 * s + j + 1)
                            act.copy(qk[:, s % 2, j * CH:(j + 1) * CH], bank[:, PJ[j % 2], :]).then_inc(S.proj_out, 1)

                    def square_qk(s):
                        act.wait_ge(S.proj_out, 8 * s + 4)
                        if s >= 1:
                            act.wait_ge(S.sumsq, s)
                        act.activation(sq[:, :], qk[:, s % 2, :], ACT.Square).then_inc(S.squared, 1)

                    def norm_qk(s):
                        act.wait_ge(S.sumsq, s + 1)
                        if s >= 2:
                            act.wait_ge(S.inv_norm, s - 1)
                        act.activation(rn[:, s % 2, :], ssq[:, s % 2, :], ACT.Sqrt).then_inc(S.norm, 1)

                    def empty_v(s):
                        if s >= 2:
                            act.wait_ge(S.av, 2 * (s - 1))
                        for w in range(WPB):
                            act.wait_ge(S.proj, 8 * s + 4 + w + 1)
                            act.copy(v[:, s % 2, w, :, :].rearrange("p h d -> p (h d)"), bank[:, PJ[w % 2], :])\
                               .then_inc(S.proj_out, 1)

                    def empty_turned(s):
                        if s >= 2:
                            act.wait_ge(S.scores, 2 * (s - 1))
                        if s >= 2:
                            act.copy(k_t[:, s % 2, :, 0:WIN], k_t[:, s % 2, :, BLK:BLK + WIN]).then_inc(S.lookback, 1)
                        for g in range(4):
                            act.wait_ge(S.misc, turn["turn", s, g] + 1)
                            src = bank[:, misc("turn", s, g), :].rearrange("p (h t) -> p h t", t=BLK)
                            if g < 2:
                                dst = q_t[:, s % 2, 4 * g:4 * g + 4, :]
                            else:
                                if s >= 2:
                                    act.wait_ge(S.lookback, s - 1)
                                dst = k_t[:, s % 2, 4 * g - 8:4 * g - 4, WIN:WIN + BLK]
                            act.copy(dst, src).then_inc(S.misc_out, 1)

                    def empty_pairs(kind, dst, s):
                        for g in range(2):
                            act.wait_ge(S.misc, turn[kind, s, g] + 1)
                            act.copy(dst[:, s % 2, 4 * g:4 * g + 4, :].rearrange("p h t -> p (h t)"),
                                     bank[:, misc(kind, s, g), :]).then_inc(S.misc_out, 1)

                    def empty_att(s):
                        if s >= 2:
                            act.wait_ge(S.misc, turn["out", s - 2, 0] + 1)
                        empty_pairs("att", att_t, s)

                    def empty_prob(s):
                        if s >= 2:
                            act.wait_ge(S.av, 2 * (s - 1))
                        empty_pairs("prob", prob_t, s)

                    def empty_out(s):
                        act.wait_ge(S.misc, turn["out", s, 0] + 1)
                        act.copy(tokens(h_mid, s), bank[:, misc("out", s, 0), 0:BLK]).then_inc(S.misc_out, 1)

                    def exponent(s):
                        act.wait_ge(S.shifted, 2 * (s + 1))
                        act.activation(prob[:, s % 2, :, :, :], prob[:, s % 2, :, :, :], ACT.Exp).then_inc(S.probs, 1)

                    for s in range(-1, SLOTS + 2):
                        if live(s + 1):
                            empty_qk(s + 1)
                        if live(s):
                            empty_turned(s)
                        if live(s - 2):
                            empty_att(s - 2)
                        if live(s - 1):
                            empty_prob(s - 1)
                        if live(s + 1):
                            square_qk(s + 1)
                        if live(s - 2):
                            empty_out(s - 2)
                        if live(s + 1):
                            norm_qk(s + 1)
                            empty_v(s + 1)
                        if live(s):
                            exponent(s)

                    def gate(c):
                        for j in range(FB):
                            n = FB * c + j
                            m = FROWS[j]
                            act.wait_ge(S.gate_mm, n + 1)
                            if n >= 2:
                                act.wait_ge(S.hidden, n - 1)
                            act.activation(fgate[0:m, n % 2, :], bank[0:m, PJ[n % 2], :], ACT.Gelu,
                                           bias=lvec[0:m, 6 + j:7 + j]).then_inc(S.gated, 1)

                    act.wait_ge(S.weights, 64)
                    for c in range(NCH):
                        act_square(act, c)
                        act_dev(act, c)
                        if c >= 1:
                            gate(c - 1)
                    gate(NCH - 1)

                @block.vector
                def _(dve):
                    def stage(s):
                        lo = PAD + (s // 2) * BLK - WIN
                        if s >= 2:
                            dve.wait_ge(S.proj, 8 * (s - 1))
                        for f, back in ((slice(0, 64), 0), (slice(64, P), 1)):
                            dve.tensor_copy(x_s[f, s % 2, :], h_in[f, s % 2, lo - back:lo - back + WIN + BLK]).then_inc(S.staged, 1)

                    def sum_squares(s):
                        dve.wait_ge(S.squared, s + 1)
                        if s >= 2:
                            dve.wait_ge(S.norm, s - 1)
                        dve.tensor_reduce(ssq[:, s % 2, :], sq[:, :].rearrange("p (h d) -> p h d", d=HD), AX.X, ALU.add)\
                           .then_inc(S.sumsq, 1)

                    def normalise(s):
                        r = rn[:, s % 2, :]
                        dve.wait_ge(S.norm, s + 1)
                        dve.tensor_scalar(r, r, 1e-12, None, ALU.max).then_inc(S.clamped, 1)
                        dve.wait_ge(S.clamped, s + 1)
                        dve.reciprocal(r, r).then_inc(S.inv_norm, 1)
                        dve.wait_ge(S.inv_norm, s + 1)
                        if s >= 1:
                            dve.wait_ge(S.rot_sin, 2 * s)
                        dve.tensor_tensor(qn[:, :].rearrange("p (h d) -> p h d", d=HD),
                                          qk[:, s % 2, :].rearrange("p (h d) -> p h d", d=HD),
                                          r.unsqueeze(2).to_broadcast([P, 2 * HEADS, HD]), ALU.mult).then_inc(S.normed, 1)
                        dve.wait_ge(S.normed, s + 1)
                        if s >= 1:
                            dve.wait_ge(S.rotated, s)
                        dve.tensor_tensor(t_cos[:, :].rearrange("p (a h d) -> p a h d", a=2, h=HEADS),
                                          qn[:, :].rearrange("p (a h d) -> p a h d", a=2, h=HEADS),
                                          cos[:, s // 2, :].rearrange("p (a d) -> p a d", a=2).unsqueeze(2)
                                          .to_broadcast([P, 2, HEADS, HD]), ALU.mult).then_inc(S.rot_cos, 1)

                    def shift_scores(s):
                        if s >= 2:
                            dve.wait_ge(S.misc, turn["prob", s - 2, 1] + 1)
                            dve.wait_ge(S.rowsum, s - 1)
                        if s >= 1:
                            dve.wait_ge(S.shifted, 2 * s)
                        for par in range(2):
                            dve.wait_ge(S.scores, 2 * s + par + 1)
                            dve.tensor_reduce(row_max[:, par, :], bank[:, SC[par], :].rearrange("p (h k) -> p h k", k=HD),
                                              AX.X, ALU.max).then_inc(S.rowmax, 1)
                        for par in range(2):
                            dve.wait_ge(S.rowmax, 2 * s + par + 1)
                            dve.tensor_tensor(prob[:, s % 2, :, par, :],
                                              bank[:, SC[par], :].rearrange("p (h k) -> p h k", k=HD),
                                              row_max[:, par, :].unsqueeze(2).to_broadcast([P, PAIRS, HD]),
                                              ALU.subtract).then_inc(S.shifted, 1)

                    def sum_probs(s):
                        r = row_sum[:, s % 2, :]
                        dve.wait_ge(S.probs, s + 1)
                        if s >= 2:
                            dve.wait_ge(S.av_out, 2 * (s - 1))
                        dve.tensor_reduce(r, prob[:, s % 2, :, :, :].rearrange("p h a k -> p (h a) k"), AX.X, ALU.add)\
                           .then_inc(S.rowsum, 1)
                        dve.wait_ge(S.rowsum, s + 1)
                        dve.reciprocal(r, r).then_inc(S.inv_sum, 1)

                    def norm_att(s):
                        dve.wait_ge(S.inv_sum, s + 1)
                        if s >= 2:
                            dve.wait_ge(S.misc, turn["att", s - 2, 1] + 1)
                        for par in range(2):
                            dve.wait_ge(S.av, 2 * s + par + 1)
                            r = row_sum[:, s % 2, :].rearrange("p (h a) -> p h a", a=2)[:, :, par:par + 1]
                            dve.tensor_tensor(att[:, s % 2, :, par, :],
                                              bank[:, AV[par], :].rearrange("p (h d) -> p h d", d=HD),
                                              r.to_broadcast([P, PAIRS, HD]), ALU.mult).then_inc(S.av_out, 1)

                    stage(0)
                    stage(1)
                    dve.wait_ge(S.scales, 3)
                    for s in range(-1, SLOTS + 2):
                        if s >= 0 and live(s + 2):
                            stage(s + 2)
                        if live(s - 1):
                            sum_probs(s - 1)
                        if live(s + 1):
                            sum_squares(s + 1)
                            normalise(s + 1)
                        if live(s):
                            shift_scores(s)
                        if live(s - 1):
                            norm_att(s - 1)

                    def shift_tokens(c):
                        if c >= 2:
                            dve.wait_ge(s_normed, c - 1)
                        lo = PAD + (c % 2) * CH
                        for f, back in ((slice(0, 64), 0), (slice(64, P), 1)):
                            dve.tensor_copy(xs2[f, c % 2, :], h_mid[f, c // 2, lo - back:lo - back + CH]).then_inc(S.xs2, 1)

                    def hidden(c):
                        for j in range(FB):
                            n = FB * c + j
                            m = FROWS[j]
                            if c >= 2 and j == 0:
                                dve.wait_ge(S.down, c - 1)
                            dve.wait_ge(S.value_mm, n + 1)
                            dve.wait_ge(S.gated, n + 1)
                            dve.scalar_tensor_tensor(out=fh[0:m, c % 2, j, :], in0=bank[0:m, MISC[n % 2], :],
                                                     scalar=lvec[0:m, 3 + j:4 + j], in1=fgate[0:m, n % 2, :],
                                                     op0=ALU.add, op1=ALU.mult).then_inc(S.hidden, 1)

                    def finish(c):
                        dve.wait_ge(S.down, c + 1)
                        dve.scalar_tensor_tensor(out=padded(h_in, c), in0=bank[:, AV[c % 2], :], scalar=lvec[:, 2:3],
                                                 in1=padded(h_mid, c), op0=ALU.add, op1=ALU.add).then_inc(S.ff_out, 1)

                    dve.wait_ge(S.misc_out, len(turn))
                    dve.wait_ge(S.weights, 64)
                    shift_tokens(0)
                    shift_tokens(1)
                    dve.wait_ge(S.xs2, 4)
                    dve_center(dve, 0)
                    for c in range(NCH):
                        if c + 1 < NCH:
                            dve_center(dve, c + 1)
                        dve_norm(dve, c)
                        if c >= 1:
                            hidden(c - 1)
                            finish(c - 1)
                        if c + 2 < NCH:
                            shift_tokens(c + 2)
                            dve.wait_ge(S.xs2, 2 * (c + 3))
                    hidden(NCH - 1)
                    finish(NCH - 1)
                    dve.wait_ge(S.ff_out, NCH)
            nc.all_engine_barrier(sems_to_clear=span)


def full_attention(nc, A, sb, sem, bank, ident, h_in, padded, x_chunk, mod):
    QB = N // P
    UNITS = B * QB
    SCALE = HD ** -0.5
    with ExitStack() as ctx:
        def buf(name, shape, dt=F32):
            return sb(f"fa_{name}", shape, dt, ctx=ctx)

        anti = buf("anti", [P, P])
        w_out = buf("w_out", [P, PAIRS, P])
        w = buf("w", [P, 3, P])
        rel = buf("rel", [P, 2, 2 * P])
        q_t = buf("q_t", [P, B, N])
        k_t = buf("k_t", [P, B, N])
        v = buf("v", [P, B, QB, P])
        neg_max = buf("neg_max", [P, 2, 2, 2])
        row_sum = buf("row_sum", [P, 2, 2])
        prob = buf("prob", [P, 2, 2, N])
        prob_t = buf("prob_t", [P, 2, 2, QB, P])
        att_all = buf("att_all", [P, PAIRS, B, N])
        y = buf("y", [P, 2, CH])

        s_load = sem("s_fa_load")
        with nc.Block() as block:
            @block.sync
            def _(sp):
                sp.dma_start(anti[:, :], A["anti"]).then_inc(s_load, 16)
                sp.dma_start(w_out[:, :, :], A["fa_wout"]).then_inc(s_load, 16)
                sp.wait_ge(s_load, 32)

        names = "w_in rel_in rel8 proj proj_out scores rowmax negmax probs inv_sum scaled turned turned_a turned_v av av_out".split()
        first = {n: sem(f"s_fa_{n}", ctx) for n in names}
        S = type("S", (), first)
        numbers = [s.num for s in first.values()]
        span = range(min(numbers), max(numbers) + 1)
        on_vector = (3,)

        with nc.Fori(0, PAIRS) as pair:
            with nc.Block(no_gpsimd_drain=True) as block:
                def wait_turned(eng, n):
                    if n % 4 in on_vector:
                        eng.wait_ge(S.turned_v, n // 4 + 1)
                    else:
                        eng.wait_ge(S.turned_a, 3 * (n // 4) + n % 4 + 1)

                def empty_turned(eng, u, which, done):
                    for i in which:
                        n = 4 * u + i
                        eng.wait_ge(S.turned, n + 1)
                        if u >= 2:
                            eng.wait_ge(S.av, u - 1)
                        dst = prob_t[:, u % 2, i // 2, 4 * (i % 2):4 * (i % 2) + 4, :].rearrange("p k q -> p (k q)")
                        src = bank[:, 4 + n % 2, :]
                        (eng.copy if done is S.turned_a else eng.tensor_copy)(dst, src).then_inc(done, 1)

                def empty_av(act, u):
                    b, qb = u // QB, u % QB
                    act.wait_ge(S.av, u + 1)
                    act.copy(att_all[:, pair, b, qb * P:(qb + 1) * P], bank[:, 6 + u % 2, 0:P]).then_inc(S.av_out, 1)

                @block.sync
                def _(sp):
                    sp.dma_start(w[:, :, :], A["fa_w"][pair]).then_inc(S.w_in, 16)
                    sp.dma_start(rel[:, :, :], A["fa_rel"][pair]).then_inc(S.rel_in, 16)
                    sp.wait_ge(S.w_in, 16)
                    sp.wait_ge(S.rel_in, 16)

                @block.tensor
                def _(pe):
                    pe.wait_ge(S.w_in, 16)
                    for b in range(B):
                        for i in range(6):
                            n = 6 * b + i
                            if n >= 8:
                                pe.wait_ge(S.proj_out, n - 7)
                            o = bank[:, n % 8, :]
                            if i < 4:
                                mm = pe.matmul(o, w[:, i // 2, :], padded(h_in, 2 * b + i % 2), start=True, stop=True)
                            else:
                                for t in range(4):
                                    lo = PAD + ((i - 4) * 4 + t) * P
                                    mm = pe.matmul(o[:, t * P:(t + 1) * P], h_in[:, b, lo:lo + P], w[:, 2, :],
                                                   start=True, stop=True)
                            mm.then_inc(S.proj, 1)

                    def scores(u):
                        b, qb = u // QB, u % QB
                        for par in range(2):
                            f = slice(64 * par, 64 * par + 64)
                            if u >= 1:
                                pe.wait_ge(S.probs, 2 * (u - 1) + par + 1)
                            for half in range(2):
                                near = qb >= 6 and half == 0
                                mm = pe.matmul(bank[:, 2 * par + half, :], q_t[f, b, qb * P:(qb + 1) * P],
                                               k_t[f, b, half * CH:(half + 1) * CH], start=True, stop=not near)
                                if near:
                                    cols = slice(P, 2 * P) if qb == 6 else slice(0, 2 * P)
                                    mm = pe.matmul(bank[:, 2 * par, 0:P * (qb - 5)], anti[:, :], rel[:, par, cols],
                                                   start=False, stop=True)
                            mm.then_inc(S.scores, 1)

                    def turn(u):
                        for par in range(2):
                            pe.wait_ge(S.scaled, 2 * u + par + 1)
                            for g in range(2):
                                n = 4 * u + 2 * par + g
                                if n >= 2:
                                    wait_turned(pe, n - 2)
                                for i in range(4):
                                    mm = pe.transpose(bank[:, 4 + n % 2, i * P:(i + 1) * P],
                                                      prob[:, u % 2, par, (4 * g + i) * P:(4 * g + i + 1) * P], ident[:, :])
                                mm.then_inc(S.turned, 1)

                    def weigh_v(u):
                        b, qb = u // QB, u % QB
                        wait_turned(pe, 4 * u + 3)
                        wait_turned(pe, 4 * u + 2)
                        if u >= 2:
                            pe.wait_ge(S.av_out, u - 1)
                        for kb in range(QB):
                            for par in range(2):
                                mm = pe.matmul(bank[64 * par:64 * par + 64, 6 + u % 2, 0:P],
                                               v[:, b, kb, 64 * par:64 * par + 64], prob_t[:, u % 2, par, kb, :],
                                               start=kb == 0, stop=kb == QB - 1)
                        mm.then_inc(S.av, 1)

                    pe.wait_ge(S.proj_out, 12)
                    pe.wait_ge(S.rel8, 2)
                    scores(0)
                    for u in range(UNITS):
                        if u + 1 < UNITS:
                            scores(u + 1)
                        turn(u)
                        if u >= 1:
                            weigh_v(u - 1)
                    weigh_v(UNITS - 1)

                @block.scalar
                def _(act):
                    for b in range(B):
                        for i in range(6):
                            n = 6 * b + i
                            act.wait_ge(S.proj, n + 1)
                            dst = ((q_t, k_t)[i // 2][:, b, (i % 2) * CH:(i % 2 + 1) * CH] if i < 4 else
                                   v[:, b, 4 * (i - 4):4 * (i - 3), :].rearrange("p t d -> p (t d)"))
                            act.copy(dst, bank[:, n % 8, :]).then_inc(S.proj_out, 1)

                    def exponent(u):
                        for par in range(2):
                            act.wait_ge(S.negmax, 2 * u + par + 1)
                            if u >= 2:
                                act.wait_ge(S.turned, 4 * (u - 2) + 2 * par + 2)
                                act.wait_ge(S.inv_sum, 2 * (u - 2) + par + 1)
                            act.activation(prob[:, u % 2, par, :], bank[:, 2 * par:2 * par + 2, :].rearrange("p a n -> p (a n)"),
                                           ACT.Exp, bias=neg_max[:, u % 2, par, 1:2], scale=SCALE,
                                           accum_out=row_sum[:, u % 2, par:par + 1]).then_inc(S.probs, 1)

                    exponent(0)
                    for u in range(UNITS):
                        if u + 1 < UNITS:
                            exponent(u + 1)
                        empty_turned(act, u, (0, 1, 2), S.turned_a)
                        if u >= 1:
                            empty_av(act, u - 1)
                    empty_av(act, UNITS - 1)

                @block.vector
                def _(dve):
                    dve.wait_ge(S.rel_in, 16)
                    for par in range(2):
                        dve.tensor_scalar(rel[:, par, 0:2 * P - 1], rel[:, par, 0:2 * P - 1], rel[:, par, 2 * P - 1:2 * P],
                                          1.0 / SCALE, ALU.subtract, ALU.mult).then_inc(S.rel8, 1)
                    dve.wait_ge(S.rel8, 2)
                    for par in range(2):
                        dve.memset(rel[:, par, 2 * P - 1:2 * P], 0.0).then_inc(S.rel8, 1)

                    def maximum(u):
                        for par in range(2):
                            m = neg_max[:, u % 2, par, :]
                            dve.wait_ge(S.scores, 2 * u + par + 1)
                            if u >= 2:
                                dve.wait_ge(S.probs, 2 * (u - 2) + par + 1)
                            dve.tensor_reduce(m[:, 0:1], bank[:, 2 * par:2 * par + 2, :].rearrange("p a n -> p (a n)"),
                                              AX.X, ALU.max).then_inc(S.rowmax, 1)
                        for par in range(2):
                            m = neg_max[:, u % 2, par, :]
                            dve.wait_ge(S.rowmax, 2 * u + par + 1)
                            dve.tensor_scalar(m[:, 1:2], m[:, 0:1], -SCALE, None, ALU.mult).then_inc(S.negmax, 1)

                    def scale_probs(u):
                        for par in range(2):
                            r = row_sum[:, u % 2, par:par + 1]
                            dve.wait_ge(S.probs, 2 * u + par + 1)
                            dve.reciprocal(r, r).then_inc(S.inv_sum, 1)
                            dve.wait_ge(S.inv_sum, 2 * u + par + 1)
                            dve.tensor_scalar(prob[:, u % 2, par, :], prob[:, u % 2, par, :], r, None, ALU.mult)\
                               .then_inc(S.scaled, 1)

                    maximum(0)
                    for u in range(UNITS):
                        scale_probs(u)
                        if u + 1 < UNITS:
                            maximum(u + 1)
                        empty_turned(dve, u, on_vector, S.turned_v)
                    dve.wait_ge(S.rel8, 4)
            nc.all_engine_barrier(sems_to_clear=span)

        s_y = sem("s_fa_y")
        s_g = sem("s_fa_gated")
        s_x = sem("s_fa_x")
        with nc.Block(no_gpsimd_drain=True) as block:
            @block.tensor
            def _(pe):
                for c in range(NCH):
                    for hp in range(PAIRS):
                        mm = pe.matmul(bank[:, c, :], w_out[:, hp, :], att_all[:, hp, c // 2, (c % 2) * CH:(c % 2 + 1) * CH],
                                       start=hp == 0, stop=hp == PAIRS - 1)
                    mm.then_inc(s_y, 1)

            @block.vector
            def _(dve):
                for c in range(NCH):
                    dve.wait_ge(s_y, c + 1)
                    dve.scalar_tensor_tensor(out=x_chunk(c), in0=bank[:, c, :], scalar=mod[:, 1, 2, c // 2:c // 2 + 1],
                                             in1=x_chunk(c), op0=ALU.mult, op1=ALU.add).then_inc(s_x, 1)
                dve.wait_ge(s_x, NCH)


def experts(nc, A, sb, sem, bank, ident, h_in, x_main, mod, out):
    with ExitStack() as ctx:
        def buf(name, shape, dt=F32):
            return sb(f"ex_{name}", shape, dt, ctx=ctx)

        gate_w = buf("gate_w", [P, EXPERTS])
        b2 = buf("b2", [EXPERTS, P])
        iota = buf("iota", [P, EXPERTS])
        logits = buf("logits", [P, TB, EXPERTS])
        top = buf("top", [P, TB, 8])
        top_i = buf("top_i", [P, TB, 8], U32)
        top_f = buf("top_f", [P, TB, 8])
        pick = buf("pick", [P, 2, TB, EXPERTS])
        wt = buf("wt", [P, 4, TB])
        cw = buf("cw", [P, TB, EXPERTS])
        cw_t = buf("cw_t", [EXPERTS, TB, P])
        gb_diag = buf("gb_diag", [P, B, P])
        gb_all = buf("gb_all", [P, B, P])
        ones = buf("ones", [P, P])
        acc = buf("acc", [P, TB, P])
        w1 = buf("w1", [P, 2, EF])
        w2 = buf("w2", [P, 2, EFB, P])
        b1 = buf("b1", [P, 2, EFB])
        cw_e = buf("cw_e", [P, 2, TB])
        hid = buf("hid", [P, 2, EFB, CH])
        y = buf("y", [P, TB, P])

        s_in = sem("s_ex_in")
        s_w = sem("s_ex_first")
        s_ones = sem("s_ex_ones")
        s_lg = sem("s_ex_logits")
        s_lo = sem("s_ex_logits_out")
        s_top = sem("s_ex_top")
        s_idx = sem("s_ex_index")
        s_idf = sem("s_ex_index_f")
        s_diff = sem("s_ex_diff")
        s_exp = sem("s_ex_exp")
        s_wt = sem("s_ex_wt")
        s_cw = sem("s_ex_cw")
        s_ct = sem("s_ex_cwt")
        s_cto = sem("s_ex_cwt_out")
        s_b2 = sem("s_ex_b2")
        s_b2o = sem("s_ex_b2_out")
        s_gb = sem("s_ex_gb")
        s_gbm = sem("s_ex_gb_mm")
        s_gbo = sem("s_ex_gb_out")

        def h_block(t):
            lo = PAD + (t % (TB // B)) * P
            return h_in[:, t // (TB // B), lo:lo + P]

        with nc.Block(no_gpsimd_drain=True) as block:
            @block.sync
            def _(sp):
                sp.dma_start(gate_w[:, :], A["gate_w"]).then_inc(s_in, 16)
                sp.dma_start(b2[:, :], A["ex_b2"]).then_inc(s_in, 16)
                sp.dma_start(iota[:, :], A["iota"]).then_inc(s_in, 16)
                sp.dma_start(w1[:, 0, :], A["ex_w1"][0]).then_inc(s_w, 16)
                sp.dma_start(w2[:, 0, :, :], A["ex_w2"][0]).then_inc(s_w, 16)
                sp.dma_start(b1[:, 0, :], A["ex_b1"][0]).then_inc(s_w, 16)
                sp.wait_ge(s_in, 48)
                sp.wait_ge(s_w, 48)

            @block.gpsimd
            def _(pool):
                pool.memset(ones[:, :], 1.0).then_inc(s_ones, 1)
                pool.wait_ge(s_ones, 1)

            @block.tensor
            def _(pe):
                pe.wait_ge(s_in, 48)
                for t in range(TB):
                    mm = pe.matmul(bank[:, 0, t * EXPERTS:(t + 1) * EXPERTS], h_block(t), gate_w[:, :], start=True, stop=True)
                mm.then_inc(s_lg, 1)
                pe.wait_ge(s_ones, 1)
                pe.wait_ge(s_gb, 2)
                for b in range(B):
                    mm = pe.matmul(bank[:, 1, b * P:(b + 1) * P], ones[:, :], gb_diag[:, b, :], start=True, stop=True)
                mm.then_inc(s_gbm, 1)
                pe.wait_ge(s_cw, 3)
                for g in range(4):
                    for i in range(4):
                        mm = pe.transpose(bank[0:EXPERTS, 2 + g % 2, i * P:(i + 1) * P], cw[:, 4 * g + i, :], ident[:, :])
                    mm.then_inc(s_ct, 1)
                    if g >= 1:
                        pe.wait_ge(s_cto, g)
                for g in range(4):
                    pe.wait_ge(s_cto, g + 1)
                    for i in range(4):
                        mm = pe.matmul(bank[:, 4 + g, i * P:(i + 1) * P], cw_t[:, 4 * g + i, :], b2[:, :], start=True, stop=True)
                    mm.then_inc(s_b2, 1)

            @block.scalar
            def _(act):
                act.wait_ge(s_diff, 1)
                act.activation(wt[:, 1, :], wt[:, 0, :], ACT.Exp).then_inc(s_exp, 1)

            @block.vector
            def _(dve):
                for b in range(B):
                    dve.tensor_scalar(gb_diag[:, b, :], ident[:, :], mod[:, 1, 5, b:b + 1], None, ALU.mult).then_inc(s_gb, 1)
                dve.wait_ge(s_lg, 1)
                dve.tensor_copy(logits[:, :, :].rearrange("p t e -> p (t e)"), bank[:, 0, 0:TB * EXPERTS]).then_inc(s_lo, 1)
                dve.wait_ge(s_lo, 1)
                for t in range(TB):
                    dve.max(top[:, t, :], logits[:, t, :]).then_inc(s_top, 1)
                dve.wait_ge(s_top, TB)
                for t in range(TB):
                    dve.max_index(top_i[:, t, :], top[:, t, :], logits[:, t, :]).then_inc(s_idx, 1)
                dve.tensor_tensor(wt[:, 0, :], top[:, :, 1], top[:, :, 0], ALU.subtract).then_inc(s_diff, 1)
                dve.wait_ge(s_idx, TB)
                dve.tensor_copy(top_f[:, :, :], top_i[:, :, :]).then_inc(s_idf, 1)
                dve.wait_ge(s_idf, 1)
                dve.wait_ge(s_in, 48)
                for k in range(2):
                    dve.tensor_tensor(pick[:, k, :, :], top_f[:, :, k:k + 1].to_broadcast([P, TB, EXPERTS]),
                                      iota[:, :].unsqueeze(1).to_broadcast([P, TB, EXPERTS]), ALU.is_equal).then_inc(s_idf, 1)
                dve.wait_ge(s_exp, 1)
                dve.tensor_scalar(wt[:, 2, :], wt[:, 1, :], 1.0, None, ALU.add).then_inc(s_wt, 1)
                dve.wait_ge(s_wt, 1)
                dve.reciprocal(wt[:, 2, :], wt[:, 2, :]).then_inc(s_wt, 1)
                dve.wait_ge(s_wt, 2)
                dve.tensor_tensor(wt[:, 3, :], wt[:, 1, :], wt[:, 2, :], ALU.mult).then_inc(s_wt, 1)
                dve.wait_ge(s_wt, 3)
                dve.wait_ge(s_idf, 3)
                for k in range(2):
                    dve.tensor_tensor(pick[:, k, :, :], pick[:, k, :, :],
                                      wt[:, 2 + k, :].unsqueeze(2).to_broadcast([P, TB, EXPERTS]), ALU.mult).then_inc(s_cw, 1)
                dve.wait_ge(s_cw, 2)
                dve.tensor_tensor(cw[:, :, :], pick[:, 0, :, :], pick[:, 1, :, :], ALU.add).then_inc(s_cw, 1)
                dve.wait_ge(s_gbm, 1)
                dve.tensor_copy(gb_all[:, :, :].rearrange("p b d -> p (b d)"), bank[:, 1, 0:B * P]).then_inc(s_gbo, 1)
                for g in range(4):
                    dve.wait_ge(s_ct, g + 1)
                    dve.tensor_copy(cw_t[:, 4 * g:4 * g + 4, :].rearrange("e t n -> e (t n)"), bank[0:EXPERTS, 2 + g % 2, :])\
                       .then_inc(s_cto, 1)
                for g in range(4):
                    dve.wait_ge(s_b2, g + 1)
                    dve.tensor_copy(acc[:, 4 * g:4 * g + 4, :].rearrange("p t d -> p (t d)"), bank[:, 4 + g, :]).then_inc(s_b2o, 1)
                dve.wait_ge(s_b2o, 4)
                dve.wait_ge(s_gbo, 1)

        names = "odd next cw_e up gelu down added".split()
        first = {n: sem(f"s_ex_{n}", ctx) for n in names}
        S = type("S", (), first)
        numbers = [s.num for s in first.values()]
        span = range(min(numbers), max(numbers) + 1)
        def padded_chunk(c):
            return h_in[:, c // 2, PAD + (c % 2) * CH:PAD + (c % 2 + 1) * CH]

        with nc.Fori(0, EXPERTS // 2) as two:
            e = 2 * two
            with nc.Block(no_gpsimd_drain=True) as block:
                @block.sync
                def _(sp):
                    sp.dma_start(w1[:, 1, :], A["ex_w1"][e + 1]).then_inc(S.odd, 16)
                    sp.dma_start(w2[:, 1, :, :], A["ex_w2"][e + 1]).then_inc(S.odd, 16)
                    sp.dma_start(b1[:, 1, :], A["ex_b1"][e + 1]).then_inc(S.odd, 16)
                    sp.wait_ge(S.odd, 48)
                    sp.wait_ge(S.down, NCH)
                    sp.dma_start(w1[:, 0, :], A["ex_w1"][e + 2]).then_inc(S.next, 16)
                    sp.dma_start(w2[:, 0, :, :], A["ex_w2"][e + 2]).then_inc(S.next, 16)
                    sp.dma_start(b1[:, 0, :], A["ex_b1"][e + 2]).then_inc(S.next, 16)
                    sp.wait_ge(S.next, 48)

                @block.tensor
                def _(pe):
                    def up(n):
                        k, c = n // NCH, n % NCH
                        if n == NCH:
                            pe.wait_ge(S.odd, 48)
                        for j in range(EFB):
                            if n >= 1:
                                pe.wait_ge(S.gelu, EFB * (n - 1) + j + 1)
                            pe.matmul(bank[:, j, :], w1[:, k, j * P:(j + 1) * P], padded_chunk(c), start=True, stop=True)\
                              .then_inc(S.up, 1)

                    def down(n):
                        k, c = n // NCH, n % NCH
                        pe.wait_ge(S.gelu, EFB * (n + 1))
                        if n >= 2:
                            pe.wait_ge(S.added, 4 * (n - 1))
                        for t in range(4):
                            for j in range(EFB):
                                mm = pe.matmul(bank[:, 4 + n % 2, t * P:(t + 1) * P], hid[:, n % 2, j, t * P:(t + 1) * P],
                                               w2[:, k, j, :], start=j == 0, stop=j == EFB - 1)
                        mm.then_inc(S.down, 1)

                    for n in range(2 * NCH):
                        up(n)
                        if n >= 1:
                            down(n - 1)
                    down(2 * NCH - 1)

                @block.scalar
                def _(act):
                    for n in range(2 * NCH):
                        if n == NCH:
                            act.wait_ge(S.odd, 48)
                        for j in range(EFB):
                            act.wait_ge(S.up, EFB * n + j + 1)
                            if n >= 2 and j == 0:
                                act.wait_ge(S.down, n - 1)
                            act.activation(hid[:, n % 2, j, :], bank[:, j, :], ACT.Gelu, bias=b1[:, n // NCH, j:j + 1])\
                               .then_inc(S.gelu, 1)

                @block.vector
                def _(dve):
                    for k in range(2):
                        dve.tensor_copy(cw_e[:, k, :], cw[:, :, e + k]).then_inc(S.cw_e, 1)
                    dve.wait_ge(S.cw_e, 2)
                    for n in range(2 * NCH):
                        k, c = n // NCH, n % NCH
                        dve.wait_ge(S.down, n + 1)
                        if n == NCH:
                            dve.wait_ge(S.added, 4 * NCH)
                        for t in range(4):
                            a = acc[:, 4 * c + t, :]
                            dve.scalar_tensor_tensor(out=a, in0=bank[:, 4 + n % 2, t * P:(t + 1) * P],
                                                     scalar=cw_e[:, k, 4 * c + t:4 * c + t + 1], in1=a,
                                                     op0=ALU.mult, op1=ALU.add).then_inc(S.added, 1)
                    dve.wait_ge(S.added, 8 * NCH)

            nc.all_engine_barrier(sems_to_clear=span)

        s_xt = sem("s_ex_x_turned")
        s_gy = sem("s_ex_gated")
        s_y = sem("s_ex_y")
        s_out = sem("s_ex_out")
        rows = out.rearrange("b (t p) d -> p (b t) d", p=P)
        with nc.Block() as block:
            @block.tensor
            def _(pe):
                for g in range(4):
                    for i in range(4):
                        t = 4 * g + i
                        mm = pe.transpose(bank[:, g, i * P:(i + 1) * P],
                                          x_main[:, t // 8, (t % 8) * P:(t % 8 + 1) * P], ident[:, :])
                    mm.then_inc(s_xt, 1)

            @block.vector
            def _(dve):
                for g in range(4):
                    o = y[:, 4 * g:4 * g + 4, :]
                    dve.tensor_tensor(o, acc[:, 4 * g:4 * g + 4, :], gb_all[:, g // 2:g // 2 + 1, :].to_broadcast([P, 4, P]),
                                      ALU.mult).then_inc(s_gy, 1)
                    dve.wait_ge(s_gy, g + 1)
                    dve.wait_ge(s_xt, g + 1)
                    dve.tensor_tensor(o, o, bank[:, g, :].rearrange("p (t d) -> p t d", d=P), ALU.add).then_inc(s_y, 1)

            @block.sync
            def _(sp):
                for g in range(4):
                    sp.wait_ge(s_y, g + 1)
                    sp.dma_start(rows[:, 4 * g:4 * g + 4, :], y[:, 4 * g:4 * g + 4, :]).then_inc(s_out, 16)
                sp.wait_ge(s_out, 64)


def _constants():
    import numpy as np
    f = np.float32
    half = np.arange(0, HD, 2, dtype=f)
    inv_freq = (f(1.0) / np.power(f(10000.0), half / f(HD))).astype(f)
    t = np.arange(N, dtype=f)
    freqs = t[:, None] * inv_freq[None, :]
    base = (half + f(0.4 * HD)) / f(1.4 * HD)
    power = (t - f(N // 2)) / f(WIN // 2)
    scale = np.power(base[None, :], power[:, None]).astype(f)
    qk = np.stack([scale * f(8.0), f(1.0) / scale], 1)
    cos = np.cos(freqs)[:, None, :] * qk
    sin = np.sin(freqs)[:, None, :] * qk
    cos = np.concatenate([cos, cos], -1).astype(f)
    sin = np.concatenate([-sin, sin], -1).astype(f)

    def blocks(a):
        return np.ascontiguousarray(a.reshape(N // P, P, 2 * HD).transpose(1, 0, 2))

    q = np.arange(P)
    key = np.arange(HD)
    i, w = q % WIN, q // WIN
    allowed = np.where(key[None, :] < WIN, key[None, :] >= i[:, None], key[None, :] - WIN <= i[:, None])
    start = allowed & ~((w[:, None] == 0) & (key[None, :] < WIN))
    mask = np.where(np.stack([start, allowed], 1), f(0), f(-1e30)).astype(f)
    eye = np.eye(P, dtype=f)
    return {
        "cos": blocks(cos), "sin": blocks(sin), "mask": mask, "ident": eye,
        "anti": np.ascontiguousarray(eye[::-1]),
        "group_mean": np.kron(np.eye(P // 8, dtype=f), np.full((8, 8), 0.125, f)).astype(f),
        "iota": np.tile(np.arange(EXPERTS, dtype=f), (P, 1)),
    }


def _layout(d):
    import numpy as np
    c = np.ascontiguousarray

    def cat(*a):
        return c(np.stack(a, 1))

    def again(a):
        return c(np.concatenate([a, a[-1:]], 0))

    L = d
    lv = np.zeros((LAYERS, P, 9), np.float32)
    lv[:, :, 0], lv[:, :, 1], lv[:, :, 2] = L["L0_ffn_ln_g"], L["L0_ffn_ln_b"], L["L0_ffn_b2"]
    b1 = L["L0_ffn_b1"]
    w2 = np.zeros((LAYERS, P, FB, P), np.float32)
    for j in range(FB):
        m = FROWS[j]
        lv[:, 0:m, 3 + j] = b1[:, j * P:j * P + m]
        lv[:, 0:m, 6 + j] = b1[:, FF + j * P:FF + j * P + m]
        w2[:, 0:m, j, :] = L["L0_ffn_W2"][:, j * P:j * P + m, :]
    rel = L["L1_attn_rel_bias"].T
    rel = np.concatenate([rel, np.repeat(rel[:, -1:], 384 - rel.shape[1], 1)], 1)
    hankel = rel[:, np.arange(P)[:, None] + np.arange(2 * P)]
    w = L["L1_attn_w_qkv"].reshape(HD, 3, PAIRS, 2, P)
    return {
        "x_t": c(L["L0_attn_x"].transpose(2, 0, 1)),
        "c_t": c(np.stack([L["L0_c"].T, L["L1_c"].T], 1)),
        "wmod": cat(L["L0_wmod"], L["L1_wmod"]),
        "tm_w": cat(*[L[f"L0_attn_W{n}_w"].T for n in "grkvo"]),
        "tm_vec": cat(*[L[f"L0_attn_W{n}_b"] for n in "grkvo"], *[L[f"L0_attn_m{n}"] for n in "grkv"],
                      L["L0_attn_w"].reshape(-1), L["L0_attn_u"].reshape(-1)),
        "lt_wqkv": again(L["L0_ffn_Wqkv"]),
        "lt_qkscale": again(np.concatenate([L["L0_ffn_q_scale"], L["L0_ffn_k_scale"]], 1)[:, None, :]),
        "lt_wo": c(L["L0_ffn_Wo"].reshape(LAYERS, PAIRS, P, P).transpose(0, 2, 1, 3)),
        "lt_w1": c(L["L0_ffn_W1"]), "lt_w2": w2, "lt_vec": lv,
        "fa_w": c(w.transpose(2, 4, 1, 3, 0).reshape(PAIRS, P, 3, P)),
        "fa_rel": c(hankel.reshape(PAIRS, 2, P, 2 * P).transpose(0, 2, 1, 3)),
        "fa_wout": c(L["L1_attn_w_out"].T.reshape(PAIRS, P, P).transpose(1, 0, 2)),
        "gate_w": c(L["L1_ffn_gate_w"]), "ex_b2": c(L["L1_ffn_b2"]),
        "ex_w1": again(L["L1_ffn_w1"]),
        "ex_w2": again(L["L1_ffn_w2"].reshape(EXPERTS, EFB, P, P).transpose(0, 2, 1, 3)),
        "ex_b1": again(L["L1_ffn_b1"].reshape(EXPERTS, EFB, P).transpose(0, 2, 1)),
    }


def kernel(**inputs):
    import numpy as _np
    import concourse.bacc as _bacc
    from concourse import mybir as _mybir
    from concourse.bass_utils import run_bass_kernel_spmd as _run

    nc = _bacc.Bacc("TRN2", target_bir_lowering=False, num_devices=1)
    host = {**_layout({k: _np.asarray(v) for k, v in inputs.items()}), **_constants()}
    arrays, aps = {}, {}
    for name, a in host.items():
        arrays[f"in_{name}_dram"] = _np.ascontiguousarray(a)
        aps[name] = nc.dram_tensor(f"in_{name}_dram", a.shape, _mybir.dt.from_np(a.dtype), kind="ExternalInput").ap()
    o = nc.dram_tensor("out_0_dram", (B, N, P), F32, kind="ExternalOutput").ap()
    build(nc, aps, o)
    r = _run(nc, [arrays], core_ids=[0])
    return r.results[0]["out_0_dram"]
```

```python
from contextlib import ExitStack

import concourse.bass as bass
import concourse.mybir as mybir

F32 = mybir.dt.float32
BF16 = mybir.dt.bfloat16
F32R = mybir.dt.float32r
U32 = mybir.dt.uint32
ALU = mybir.AluOpType
ACT = mybir.ActivationFunctionType
AX = mybir.AxisListType

P = 128
B = 2
N = 1024
TOK = B * N
CH = 512
NCH = TOK // CH
PAD = 33

LAYERS = 6
HEADS = 16
HD = 64
PAIRS = HEADS // 2
WIN = 32
BLK = 128
WPB = BLK // WIN
SLOTS = TOK // BLK
INNER = HEADS * HD
FF = 341
FB = 3
FROWS = [128, 128, FF - 256]

EXPERTS = 8
EF = 512
EFB = EF // P
TB = TOK // P
LN_EPS = 1e-5


def build(nc, A, out):
    with ExitStack() as whole:
        def sb(name, shape, dt=F32, ctx=whole):
            return ctx.enter_context(nc.sbuf_tensor(name, shape, dt))

        def sem(name, ctx=whole):
            return ctx.enter_context(nc.semaphore(name))

        bank = whole.enter_context(nc.psum_tensor("bank", [P, 8, CH], F32))

        x_main = sb("x_main", [P, B, N])
        h_in = sb("h_in", [P, B, PAD + N])
        h_mid = sb("h_mid", [P, B, PAD + N])
        ident = sb("ident", [P, P])
        mean_w = sb("mean_w", [P, P])
        eps = sb("eps", [P, 1])
        mod = sb("mod", [P, 2, 6, B])
        gate_a = sb("gate_a", [P, 2, 2, B])

        def x_chunk(c):
            return x_main[:, c // 2, (c % 2) * CH:(c % 2 + 1) * CH]

        def padded(t, c):
            return t[:, c // 2, PAD + (c % 2) * CH:PAD + (c % 2 + 1) * CH]

        with ExitStack() as ctx:
            wmod = sb("wmod", [P, 2, 6 * P], ctx=ctx)
            c_t = sb("c_t", [P, 2, B], ctx=ctx)
            c_silu = sb("c_silu", [P, 2, B], ctx=ctx)
            s_in = sem("s_in")
            s_const = sem("s_const")
            s_silu = sem("s_silu")
            s_mod_mm = sem("s_mod_mm")
            s_mod = sem("s_mod")
            block = ctx.enter_context(nc.Block())

            @block.sync
            def _(sp):
                sp.dma_start(c_t[:, :, :], A["c_t"]).then_inc(s_in, 16)
                sp.dma_start(wmod[:, :, :], A["wmod"]).then_inc(s_in, 16)
                sp.dma_start(x_main[:, :, :], A["x_t"]).then_inc(s_in, 16)
                sp.dma_start(ident[:, :], A["ident"]).then_inc(s_in, 16)
                sp.wait_ge(s_in, 64)

            @block.gpsimd
            def _(pool):
                pool.memset(mean_w[:, :], 1.0 / P).then_inc(s_const, 1)
                pool.memset(eps[:, :], LN_EPS).then_inc(s_const, 1)
                pool.memset(h_in[:, :, 0:PAD], 0.0).then_inc(s_const, 1)
                pool.memset(h_mid[:, :, 0:PAD], 0.0).then_inc(s_const, 1)
                pool.wait_ge(s_const, 4)

            @block.scalar
            def _(act):
                act.wait_ge(s_in, 64)
                act.activation(c_silu[:, :, :], c_t[:, :, :], ACT.Silu).then_inc(s_silu, 1)

            @block.tensor
            def _(pe):
                pe.wait_ge(s_silu, 1)
                for la in range(2):
                    for j in range(6):
                        mm = pe.matmul(bank[:, 0, (la * 6 + j) * B:(la * 6 + j + 1) * B],
                                       wmod[:, la, j * P:(j + 1) * P], c_silu[:, la, :], start=True, stop=True)
                mm.then_inc(s_mod_mm, 1)

            @block.vector
            def _(dve):
                flat = mod[:, :, :, :].rearrange("p l j b -> p (l j b)")
                dve.wait_ge(s_mod_mm, 1)
                dve.tensor_copy(flat, bank[:, 0, 0:24]).then_inc(s_mod, 1)
                dve.wait_ge(s_mod, 1)
                n = 1
                for la in range(2):
                    for i, j in enumerate((2, 5)):
                        g = mod[:, la, j, :]
                        a = gate_a[:, la, i, :]
                        dve.tensor_scalar(a, g, 0.0, 2.0, ALU.is_ge, ALU.mult).then_inc(s_mod, 1)
                        dve.wait_ge(s_mod, n + 1)
                        dve.tensor_scalar(a, a, -1.0, None, ALU.add).then_inc(s_mod, 1)
                        dve.wait_ge(s_mod, n + 2)
                        dve.tensor_tensor(g, g, a, ALU.mult).then_inc(s_mod, 1)
                        dve.wait_ge(s_mod, n + 3)
                        dve.scalar_tensor_tensor(out=g, in0=g, scalar=0.25, in1=a, op0=ALU.max, op1=ALU.mult)\
                           .then_inc(s_mod, 1)
                        dve.wait_ge(s_mod, n + 4)
                        dve.tensor_scalar(mod[:, la, j - 1, :], mod[:, la, j - 1, :], 1.0, None,
                                          ALU.add).then_inc(s_mod, 1)
                        dve.wait_ge(s_mod, n + 5)
                        n += 5

        def modulated_norm(tag, la, first, dst):
            with ExitStack() as ctx:
                centered = sb(f"{tag}_centered", [P, NCH, CH], ctx=ctx)
                squares = sb(f"{tag}_squares", [P, NCH, CH], ctx=ctx)
                rstd = sb(f"{tag}_rstd", [P, NCH, CH], ctx=ctx)
                names = "mean centered squared var ln rstd scaled out".split()
                first_sems = {n: sem(f"s_{tag}_{n}", ctx) for n in names}
                S = type("S", (), first_sems)
                numbers = [s.num for s in first_sems.values()]
                with nc.Block(no_gpsimd_drain=True) as block:
                    @block.tensor
                    def _(pe):
                        for c in range(NCH):
                            pe.matmul(bank[:, c, :], mean_w[:, :], x_chunk(c), start=True, stop=True).then_inc(S.mean, 1)
                        for c in range(NCH):
                            pe.wait_ge(S.squared, c + 1)
                            pe.matmul(bank[:, 4 + c, :], mean_w[:, :], squares[:, c, :], start=True, stop=True)\
                              .then_inc(S.var, 1)

                    @block.scalar
                    def _(act):
                        for c in range(NCH):
                            act.wait_ge(S.centered, c + 1)
                            act.activation(squares[:, c, :], centered[:, c, :], ACT.Square).then_inc(S.squared, 1)
                        for c in range(NCH):
                            act.wait_ge(S.var, c + 1)
                            act.activation(rstd[:, c, :], bank[:, 4 + c, :], ACT.Ln, bias=eps[:, :]).then_inc(S.ln, 1)
                        for c in range(NCH):
                            act.wait_ge(S.ln, c + 1)
                            act.activation(rstd[:, c, :], rstd[:, c, :], ACT.Exp, scale=-0.5).then_inc(S.rstd, 1)

                    @block.vector
                    def _(dve):
                        for c in range(NCH):
                            dve.wait_ge(S.mean, c + 1)
                            dve.tensor_tensor(centered[:, c, :], x_chunk(c), bank[:, c, :], ALU.subtract).then_inc(S.centered, 1)
                        for c in range(NCH):
                            dve.wait_ge(S.rstd, c + 1)
                            dve.scalar_tensor_tensor(out=centered[:, c, :], in0=centered[:, c, :],
                                                     scalar=mod[:, la, first + 1, c // 2:c // 2 + 1], in1=rstd[:, c, :],
                                                     op0=ALU.mult, op1=ALU.mult).then_inc(S.scaled, 1)
                            dve.wait_ge(S.scaled, c + 1)
                            dve.tensor_scalar(dst(c), centered[:, c, :], mod[:, la, first, c // 2:c // 2 + 1], None,
                                              ALU.add).then_inc(S.out, 1)
                        dve.wait_ge(S.out, NCH)
                nc.all_engine_barrier(sems_to_clear=range(min(numbers), max(numbers) + 1))

        time_mixing(nc, A, sb, sem, bank, x_main, x_chunk, eps, mod, modulated_norm, h_mid)
        modulated_norm("ln_l0b", 0, 3, lambda c: padded(h_in, c))
        local_transformer(nc, A, sb, sem, bank, ident, mean_w, eps, h_in, h_mid, padded)
        add_gated(nc, sb, sem, x_chunk, mod, 0, lambda c: padded(h_in, c))
        modulated_norm("ln_l1a", 1, 0, lambda c: padded(h_in, c))
        full_attention(nc, A, sb, sem, bank, ident, h_in, padded, x_chunk, mod)
        modulated_norm("ln_l1b", 1, 3, lambda c: padded(h_in, c))
        experts(nc, A, sb, sem, bank, ident, h_in, x_main, mod, out)


def time_mixing(nc, A, sb, sem, bank, x_main, x_chunk, eps, mod, modulated_norm, h_mid):
    with ExitStack() as ctx:
        h = sb("tm_h", [P, B, 1 + N], ctx=ctx)
        modulated_norm("ln_l0a", 0, 0, lambda c: h[:, c // 2, 1 + (c % 2) * CH:1 + (c % 2 + 1) * CH])
        w = sb("tm_w", [P, 5, P], ctx=ctx)
        vec = sb("tm_vec", [P, 11], ctx=ctx)
        group_mean = sb("tm_group_mean", [P, P], ctx=ctx)
        diff = sb("tm_diff", [P, 2, CH], ctx=ctx)
        mix = sb("tm_mix", [P, 2, 4, CH], ctx=ctx)
        gate = sb("tm_gate", [P, B, N], ctx=ctx)
        recv = sb("tm_recv", [P, B, N], ctx=ctx)
        key = sb("tm_key", [P, 2, CH], ctx=ctx)
        kv = sb("tm_kv", [P, B, N], ctx=ctx)
        acc = sb("tm_acc", [P, B, N], ctx=ctx)
        decay = sb("tm_decay", [P, 2], ctx=ctx)
        s_w = sem("s_tm_weights")
        s_wrap = sem("s_tm_wrap")
        s_diff = sem("s_tm_diff")
        s_mix = sem("s_tm_mix")
        s_proj = sem("s_tm_proj")
        s_gate = sem("s_tm_gate")
        s_key = sem("s_tm_key")
        s_recv = sem("s_tm_recv")
        s_kv = sem("s_tm_kv")
        s_decay = sem("s_tm_decay")

        def at(t, c):
            return t[:, c // 2, (c % 2) * CH:(c % 2 + 1) * CH]

        def shifted(c):
            return h[:, c // 2, (c % 2) * CH:(c % 2 + 1) * CH]

        def straight(c):
            return h[:, c // 2, 1 + (c % 2) * CH:1 + (c % 2 + 1) * CH]

        with nc.Block(no_gpsimd_drain=True) as block:
            @block.sync
            def _(sp):
                sp.dma_start(w[:, :, :], A["tm_w"]).then_inc(s_w, 16)
                sp.dma_start(vec[:, :], A["tm_vec"]).then_inc(s_w, 16)
                sp.dma_start(group_mean[:, :], A["group_mean"]).then_inc(s_w, 16)
                sp.wait_ge(s_w, 48)

            @block.scalar
            def _(act):
                act.copy(h[:, :, 0:1], h[:, :, N:N + 1]).then_inc(s_wrap, 1)
                act.wait_ge(s_w, 48)
                act.activation(decay[:, 0:1], vec[:, 9:10], ACT.Exp).then_inc(s_decay, 1)
                act.wait_ge(s_decay, 1)
                act.activation(decay[:, 1:2], decay[:, 0:1], ACT.Exp, scale=-1.0).then_inc(s_decay, 1)
                act.wait_ge(s_decay, 2)
                for c in range(NCH):
                    q = 4 * (c % 2)
                    act.wait_ge(s_proj, 4 * c + 3)
                    if c >= 2:
                        act.wait_ge(s_kv, c - 1)
                    act.activation(key[:, c % 2, :], bank[:, q + 2, :], ACT.Identity, bias=vec[:, 2:3]).then_inc(s_key, 1)
                    act.activation(at(recv, c), bank[:, q + 1, :], ACT.Identity, bias=vec[:, 1:2]).then_inc(s_recv, 1)
                    act.activation(at(gate, c), bank[:, q, :], ACT.Sigmoid, bias=vec[:, 0:1]).then_inc(s_gate, 1)
                act.wait_ge(s_gate, NCH)
                act.wait_ge(s_recv, NCH)

            @block.vector
            def _(dve):
                dve.wait_ge(s_w, 48)
                dve.wait_ge(s_wrap, 1)
                def mixes(c):
                    if c >= 2:
                        dve.wait_ge(s_mix, 4 * (c - 1))
                    dve.tensor_tensor(diff[:, c % 2, :], straight(c), shifted(c), ALU.subtract).then_inc(s_diff, 1)
                    dve.wait_ge(s_diff, c + 1)
                    if c >= 2:
                        dve.wait_ge(s_proj, 4 * (c - 1))
                    for i in range(4):
                        dve.scalar_tensor_tensor(out=mix[:, c % 2, i, :], in0=diff[:, c % 2, :],
                                                 scalar=vec[:, 5 + i:6 + i], in1=shifted(c),
                                                 op0=ALU.mult, op1=ALU.add).then_inc(s_mix, 1)

                mixes(0)
                for c in range(NCH):
                    if c + 1 < NCH:
                        mixes(c + 1)
                    dve.wait_ge(s_key, c + 1)
                    dve.wait_ge(s_proj, 4 * c + 4)
                    dve.scalar_tensor_tensor(out=at(kv, c), in0=bank[:, 4 * (c % 2) + 3, :], scalar=vec[:, 3:4],
                                             in1=key[:, c % 2, :], op0=ALU.add, op1=ALU.mult).then_inc(s_kv, 1)
                dve.wait_ge(s_kv, NCH)

            @block.tensor
            def _(pe):
                pe.wait_ge(s_w, 48)
                for c in range(NCH):
                    if c >= 2:
                        pe.wait_ge(s_gate, c - 1)
                        pe.wait_ge(s_kv, c - 1)
                    for i in range(4):
                        pe.wait_ge(s_mix, 4 * c + i + 1)
                        pe.matmul(bank[:, 4 * (c % 2) + i, :], w[:, i, :], mix[:, c % 2, i, :],
                                  start=True, stop=True).then_inc(s_proj, 1)

        s_scan = sem("s_tm_scan")
        s_wkv = sem("s_tm_wkv")
        s_rw = sem("s_tm_rw")
        s_mean = sem("s_tm_gmean")
        s_cen = sem("s_tm_gcentered")
        s_sq = sem("s_tm_gsquares")
        s_var = sem("s_tm_gvar")
        s_ln = sem("s_tm_gln")
        s_rstd = sem("s_tm_grstd")
        s_nrm = sem("s_tm_gnorm")
        s_gated = sem("s_tm_gated")
        s_o = sem("s_tm_o")
        s_og = sem("s_tm_ogated")
        s_x = sem("s_tm_x")
        sq, dev = mix[:, 0, :, :], mix[:, 1, :, :]
        og = diff
        with nc.Block(no_gpsimd_drain=True) as block:
            @block.vector
            def _(dve):
                for b in range(B):
                    dve.tensor_tensor_scan(acc[:, b, :], decay[:, 1:2].to_broadcast([P, N]), kv[:, b, :], 0.0,
                                           ALU.mult, ALU.add).then_inc(s_scan, 1)
                for c in range(NCH):
                    dve.wait_ge(s_scan, c // 2 + 1)
                    dve.scalar_tensor_tensor(out=at(acc, c), in0=at(kv, c), scalar=vec[:, 10:11], in1=at(acc, c),
                                             op0=ALU.mult, op1=ALU.add).then_inc(s_wkv, 1)
                    dve.wait_ge(s_wkv, c + 1)
                    dve.tensor_tensor(at(recv, c), at(recv, c), at(acc, c), ALU.mult).then_inc(s_rw, 1)
                for c in range(NCH):
                    dve.wait_ge(s_mean, c + 1)
                    dve.tensor_tensor(at(recv, c), at(recv, c), bank[:, c, :], ALU.subtract).then_inc(s_cen, 1)
                for c in range(NCH):
                    dve.wait_ge(s_rstd, c + 1)
                    dve.tensor_tensor(at(recv, c), at(recv, c), dev[:, c, :], ALU.mult).then_inc(s_nrm, 1)
                    dve.wait_ge(s_nrm, c + 1)
                    dve.tensor_tensor(at(recv, c), at(recv, c), at(gate, c), ALU.mult).then_inc(s_gated, 1)
                for c in range(NCH):
                    dve.wait_ge(s_o, c + 1)
                    if c >= 2:
                        dve.wait_ge(s_x, c - 1)
                    dve.tensor_scalar(og[:, c % 2, :], bank[:, c, :], vec[:, 4:5], mod[:, 0, 2, c // 2:c // 2 + 1],
                                      ALU.add, ALU.mult).then_inc(s_og, 1)
                    dve.wait_ge(s_og, c + 1)
                    dve.tensor_tensor(x_chunk(c), x_chunk(c), og[:, c % 2, :], ALU.add).then_inc(s_x, 1)
                dve.wait_ge(s_x, NCH)

            @block.scalar
            def _(act):
                for c in range(NCH):
                    act.wait_ge(s_cen, c + 1)
                    act.activation(sq[:, c, :], at(recv, c), ACT.Square).then_inc(s_sq, 1)
                for c in range(NCH):
                    act.wait_ge(s_var, c + 1)
                    act.activation(dev[:, c, :], bank[:, 4 + c, :], ACT.Ln, bias=eps[:, :]).then_inc(s_ln, 1)
                for c in range(NCH):
                    act.wait_ge(s_ln, c + 1)
                    act.activation(dev[:, c, :], dev[:, c, :], ACT.Exp, scale=-0.5).then_inc(s_rstd, 1)

            @block.tensor
            def _(pe):
                for c in range(NCH):
                    pe.wait_ge(s_rw, c + 1)
                    pe.matmul(bank[:, c, :], group_mean[:, :], at(recv, c), start=True, stop=True).then_inc(s_mean, 1)
                for c in range(NCH):
                    pe.wait_ge(s_sq, c + 1)
                    pe.matmul(bank[:, 4 + c, :], group_mean[:, :], sq[:, c, :], start=True, stop=True).then_inc(s_var, 1)
                for c in range(NCH):
                    pe.wait_ge(s_gated, c + 1)
                    pe.matmul(bank[:, c, :], w[:, 4, :], at(recv, c), start=True, stop=True).then_inc(s_o, 1)


def add_gated(nc, sb, sem, x_chunk, mod, la, src):
    s_x = sem(f"s_gated{la}")
    with nc.Block(no_gpsimd_drain=True) as block:
        @block.vector
        def _(dve):
            for c in range(NCH):
                dve.scalar_tensor_tensor(out=x_chunk(c), in0=src(c), scalar=mod[:, la, 5, c // 2:c // 2 + 1],
                                         in1=x_chunk(c), op0=ALU.mult, op1=ALU.add).then_inc(s_x, 1)
            dve.wait_ge(s_x, NCH)


def local_transformer(nc, A, sb, sem, bank, ident, mean_w, eps, h_in, h_mid, padded):
    with ExitStack() as ctx:
        def buf(name, shape, dt=F32):
            return sb(f"lt_{name}", shape, dt, ctx=ctx)

        XS = 3
        w_high = buf("w_high", [P, 3 * INNER], F32R)
        w_low = buf("w_low", [P, 3 * INNER], F32R)
        w_o = buf("w_o", [P, PAIRS, P])
        w_1 = buf("w_1", [P, 2 * FF])
        w_2 = buf("w_2", [P, FB, P])
        lvec = buf("lvec", [P, 9])
        qk_scale = buf("qk_scale", [P, 2, HD])
        cos = buf("cos", [P, SLOTS // 2, 2 * HD])
        sin = buf("sin", [P, SLOTS // 2, 2 * HD])
        mask_f = buf("mask_f", [P, 2, HD])
        mask = buf("mask", [P, 2, PAIRS * HD], BF16)
        ident_b = buf("ident_b", [P, P], BF16)
        x_high = buf("x_high", [P, XS, BLK], F32R)
        x_low = buf("x_low", [P, XS, BLK], F32R)
        qk = buf("qk", [P, 2, 2 * INNER])
        sq = buf("sq", [P, 2 * INNER])
        ssq = buf("ssq", [P, 2, 2 * HEADS])
        rn = buf("rn", [P, 2, 2 * HEADS])
        t_sin = buf("t_sin", [P, 2 * INNER])
        qr = buf("qr", [P, 2, 2 * INNER])
        q_t = buf("q_t", [P, 2, PAIRS, BLK])
        k_t = buf("k_t", [P, 2, PAIRS, WIN + BLK])
        v_tok = buf("v_tok", [P, 2, 2, PAIRS * HD])
        v = buf("v", [P, 2, WPB, PAIRS, HD])
        w_raw = v[:, :, :, :, :].rearrange("p a w h d -> p (a w h d)")[:, 0:3 * INNER]
        row_max = buf("row_max", [P, 2, PAIRS])
        prob = buf("prob", [P, 2, PAIRS, 2, HD])
        row_sum = buf("row_sum", [P, 2, HEADS])
        prob_t = buf("prob_t", [P, 2, PAIRS, BLK])
        att = buf("att", [P, 2, PAIRS, 2, HD])
        att_t = buf("att_t", [P, 2, PAIRS, BLK])
        f_squares = sq[:, 0:1024].rearrange("p (r n) -> p r n", r=2)
        f_x = sq[:, 1024:2048].rearrange("p (r n) -> p r n", r=2)
        f_norm = qk[:, 0, :].rearrange("p (c n) -> p c n", c=NCH)
        f_rstd = qk[:, 1, :].rearrange("p (c n) -> p c n", c=NCH)
        f_gate = t_sin[:, 0:1024].rearrange("p (r n) -> p r n", r=2)
        f_hid = qr[:, :, :].rearrange("p r (j n) -> p r j n", j=4)

        PJ = (0, 1)
        SC = (2, 3)
        AV = (4, 5)
        MISC = (6, 7)
        ORDER = (0, 2, 1, 3)
        STAT = PJ + SC
        GATE = (PJ[0], AV[0])
        VALUE = (PJ[1], AV[1])

        s_tab = sem("s_lt_tables")
        s_cast = sem("s_lt_cast")
        s_w0 = sem("s_lt_first_weights")
        s_scales0 = sem("s_lt_first_scales")
        s_high0 = sem("s_lt_first_w_high")
        s_low0 = sem("s_lt_first_w_low")

        def scale_tables(pool, done):
            pool.tensor_tensor(cos[:, :, :], cos[:, :, :],
                               qk_scale[:, :, :].rearrange("p a d -> p (a d)").unsqueeze(1)
                               .to_broadcast([P, SLOTS // 2, 2 * HD]), ALU.mult).then_inc(done, 1)
            tab = sin[:, :, :].rearrange("p t (a d) -> p t a d", a=2)
            for i in range(2):
                o = slice(32 * i, 32 * i + 32)
                other = slice(32 - 32 * i, 64 - 32 * i)
                pool.tensor_tensor(tab[:, :, :, o], tab[:, :, :, o],
                                   qk_scale[:, :, other].unsqueeze(1).to_broadcast([P, SLOTS // 2, 2, 32]),
                                   ALU.mult).then_inc(done, 1)
            pool.wait_ge(done, 3)

        def split_high(act, j, done):
            act.copy(w_high[:, j * CH:(j + 1) * CH], w_raw[:, j * CH:(j + 1) * CH]).then_inc(done, 1)

        def split_low(dve, j, high_done, done):
            dve.wait_ge(high_done, j + 1)
            dve.tensor_tensor(w_low[:, j * CH:(j + 1) * CH], w_raw[:, j * CH:(j + 1) * CH],
                              w_high[:, j * CH:(j + 1) * CH].bitcast(F32), ALU.subtract).then_inc(done, 1)

        with nc.Block() as block:
            @block.gpsimd
            def _(pool):
                pool.wait_ge(s_tab, 48)
                pool.wait_ge(s_w0, 32)
                scale_tables(pool, s_scales0)

            @block.scalar
            def _(act):
                act.wait_ge(s_w0, 32)
                for j in range(6):
                    split_high(act, j, s_high0)

            @block.sync
            def _(sp):
                sp.dma_start(cos[:, :, :], A["cos"]).then_inc(s_tab, 16)
                sp.dma_start(sin[:, :, :], A["sin"]).then_inc(s_tab, 16)
                sp.dma_start(mask_f[:, :, :], A["mask"]).then_inc(s_tab, 16)
                sp.dma_start(w_raw, A["lt_wqkv"][0]).then_inc(s_w0, 16)
                sp.dma_start(qk_scale[:, :, :].rearrange("p a d -> p (a d)"),
                             A["lt_qkscale"][0].to_broadcast([P, 2 * HD])).then_inc(s_w0, 16)
                sp.wait_ge(s_tab, 48)
                sp.wait_ge(s_w0, 32)

            @block.vector
            def _(dve):
                dve.wait_ge(s_tab, 48)
                for i in range(2):
                    dve.tensor_copy(mask[:, i, :].rearrange("p (a k) -> p a k", a=PAIRS),
                                    mask_f[:, i:i + 1, :].to_broadcast([P, PAIRS, HD])).then_inc(s_cast, 1)
                dve.tensor_copy(ident_b[:, :], ident[:, :]).then_inc(s_cast, 1)
                dve.wait_ge(s_cast, 3)
                dve.wait_ge(s_w0, 32)
                for j in range(6):
                    split_low(dve, j, s_high0, s_low0)
                dve.wait_ge(s_low0, 6)

        names = ("weights next_tables next_w cleared scales w_high w_low staged_high staged look v_in_even v_in_odd v_out proj proj_out squared squared_first sumsq sumsq_first norm clamped inv_norm normed rot_cos rot_sin "
                 "rotated rotated_first lookback misc misc_out out_done scores rowmax shifted probs rowsum inv_sum av av_out "
                 "f_shift f_mean f_centered f_squared f_var f_ln f_rstd f_scaled f_normed gate_mm value_mm gated hidden down ff_out").split()
        first = {n: sem(f"s_lt_{n}", ctx) for n in names}
        S = type("S", (), first)
        numbers = [s.num for s in first.values()]
        span = range(min(numbers), max(numbers) + 1)

        turn = {}
        for s in range(-1, SLOTS + 2):
            for kind, of, groups in (("turn", s, 4), ("att", s - 2, 2), ("prob", s - 1, 2), ("out", s - 2, 1)):
                if 0 <= of < SLOTS:
                    for g in range(groups):
                        turn[kind, of, g] = len(turn)

        def misc(kind, s, g):
            return MISC[turn[kind, s, g] % 2]

        emptied = []
        for kind, s, g in turn:
            who = "v" if kind == "out" else "a"
            emptied.append((who, 1 + sum(w == who for w, _ in emptied)))

        def wait_misc(eng, n):
            who, count = emptied[n]
            eng.wait_ge(S.out_done if who == "v" else S.misc_out, count)

        def live(s):
            return 0 <= s < SLOTS

        pj = {}
        for s in range(-2, SLOTS):
            for kind, of, banks in (("qk", s + 2, 4), ("v", s + 1, 2)):
                if live(of):
                    for i in range(banks):
                        pj[kind, of, i] = len(pj)

        def tokens(t, s):
            lo = PAD + (s // 2) * BLK
            return t[:, s % 2, lo:lo + BLK]

        def v_in(s):
            return (S.v_in_even, S.v_in_odd)[s % 2]

        def wait_v_in(eng, s):
            eng.wait_ge(v_in(s), 8 * 16 * (s // 2 + 1))

        def wait_rotated(eng, s):
            if s == 0:
                eng.wait_ge(S.rotated_first, 2)
            else:
                eng.wait_ge(S.rotated, s)

        def wait_emptied(eng, u):
            kind, s, i = list(pj)[u]
            if kind == "qk":
                eng.wait_ge(S.proj_out, 4 * s + i + 1)
            else:
                eng.wait_ge(S.v_out, 2 * s + i + 1)

        qk_halves = (slice(0, 2 * CH), slice(2 * CH, 4 * CH))

        with nc.Fori(0, LAYERS) as layer:
            with nc.Block(no_gpsimd_drain=True) as block:
                @block.sync
                def _(sp):
                    sp.dma_start(w_o[:, :, :], A["lt_wo"][layer]).then_inc(S.weights, 16)
                    sp.dma_start(w_1[:, :], A["lt_w1"][layer]).then_inc(S.weights, 16)
                    sp.dma_start(w_2[:, :, :], A["lt_w2"][layer]).then_inc(S.weights, 16)
                    sp.dma_start(lvec[:, :], A["lt_vec"][layer]).then_inc(S.weights, 16)
                    for s in range(SLOTS):
                        sp.wait_ge(S.v_out, 2 * (s + 1))
                        for par in range(2):
                            lo = HD * par
                            if s >= 2:
                                if par == 0:
                                    sp.wait_ge(S.av, 2 * (s - 1))
                                sp.dma_start(v[lo:lo + WIN, s % 2, 0, :, :], v[lo + WIN:lo + 2 * WIN, s % 2, WPB - 1, :, :])\
                                  .then_inc(S.look, 16)
                        for par in range(2):
                            lo = HD * par
                            src = v_tok[:, s % 2, par, :].rearrange("p (h d) -> p h d", d=HD)
                            sp.dma_start(v[lo + WIN:lo + 2 * WIN, s % 2, 0, :, :], src[0:WIN]).then_inc(v_in(s), 16)
                            for w in range(1, WPB):
                                if par == 0 and w == WPB - 1 and s >= 2:
                                    sp.wait_ge(S.look, 32 * (s - 1))
                                sp.dma_start(v[lo:lo + 2 * WIN, s % 2, w, :, :], src[WIN * (w - 1):WIN * (w + 1)])\
                                  .then_inc(v_in(s), 16)
                    sp.dma_start(qk_scale[:, :, :].rearrange("p a d -> p (a d)"),
                                 A["lt_qkscale"][layer + 1].to_broadcast([P, 2 * HD])).then_inc(S.next_tables, 16)
                    sp.wait_ge(S.rot_cos, SLOTS)
                    sp.wait_ge(S.rot_sin, 2 * SLOTS)
                    sp.dma_start(cos[:, :, :], A["cos"]).then_inc(S.next_tables, 16)
                    sp.dma_start(sin[:, :, :], A["sin"]).then_inc(S.next_tables, 16)
                    sp.wait_ge(S.av, 2 * SLOTS)
                    wait_v_in(sp, SLOTS - 2)
                    wait_v_in(sp, SLOTS - 1)
                    sp.dma_start(w_raw, A["lt_wqkv"][layer + 1]).then_inc(S.next_w, 16)
                    sp.wait_ge(S.next_tables, 48)
                    sp.wait_ge(S.next_w, 16)
                    sp.wait_ge(S.weights, 64)

                @block.gpsimd
                def _(pool):
                    pool.memset(k_t[:, :, :, 0:WIN], 0.0).then_inc(S.cleared, 1)
                    for n in range(SLOTS):
                        if live(n):
                            pool.wait_ge(S.normed, n + 1)
                            if n >= 1:
                                wait_rotated(pool, n - 1)
                            src = qk[:, n % 2, :].rearrange("p (a h i d) -> p a h i d", a=2, h=HEADS, i=2)
                            dst = t_sin[:, :].rearrange("p (a h i d) -> p a h i d", a=2, h=HEADS, i=2)
                            tab = sin[:, n // 2, :].rearrange("p (a i d) -> p a i d", a=2, i=2)
                            for i in range(2 if n >= 1 else 1):
                                pool.tensor_tensor(dst[:, :, :, i, :], src[:, :, :, 1 - i, :],
                                                   tab[:, :, i, :].unsqueeze(2).to_broadcast([P, 2, HEADS, 32]),
                                                   ALU.mult).then_inc(S.rot_sin, 1)
                            if n >= 1:
                                pool.wait_ge(S.rot_cos, n + 1)
                                pool.wait_ge(S.rot_sin, 2 * (n + 1))
                                pool.tensor_tensor(qr[:, n % 2, :], qr[:, n % 2, :], t_sin[:, :], ALU.add).then_inc(S.rotated, 1)
                    pool.wait_ge(S.next_tables, 48)
                    scale_tables(pool, S.scales)

                @block.tensor
                def _(pe):
                    def free_misc(kind, s, g):
                        n = turn[kind, s, g]
                        if n >= 2:
                            wait_misc(pe, n - 2)

                    def project(s, u, col):
                        if u >= 2:
                            wait_emptied(pe, u - 2)
                        o = bank[:, PJ[u % 2], :]
                        pe.matmul(o, x_high[:, s % XS, :], w_high[:, col:col + CH], start=True, stop=False)
                        pe.matmul(o, x_high[:, s % XS, :], w_low[:, col:col + CH], start=False, stop=False)
                        pe.matmul(o, x_low[:, s % XS, :], w_high[:, col:col + CH], start=False, stop=True).then_inc(S.proj, 1)

                    def project_qk(s, j):
                        if j == 0:
                            pe.wait_ge(S.staged, 2 * (s + 1))
                        project(s, pj["qk", s, j], j * CH)

                    def project_v(s, par):
                        project(s, pj["v", s, par], (4 + par) * CH)

                    def turn_qk(s, g):
                        if s == 0 and g == 0:
                            pe.wait_ge(S.rotated_first, 1)
                        elif g == 0 or (s == 0 and g == 2):
                            wait_rotated(pe, s)
                        free_misc("turn", s, g)
                        for i in range(4):
                            mm = pe.transpose(bank[:, misc("turn", s, g), i * P:(i + 1) * P],
                                              qr[:, s % 2, (4 * g + i) * P:(4 * g + i + 1) * P], ident[:, :])
                        mm.then_inc(S.misc, 1)

                    def scores(s, par):
                        if par == 0:
                            wait_misc(pe, turn["turn", s, 3])
                            if s < 2:
                                pe.wait_ge(S.cleared, 1)
                        if s >= 1:
                            pe.wait_ge(S.shifted, 2 * s - 1 + par)
                        pe.matmul(bank[:, SC[par], :], ident_b[:, :], mask[:, 0 if s < 2 else 1, :],
                                  start=True, stop=False, skip_group_check=True)
                        f = slice(64 * par, 64 * par + 64)
                        for w in range(WPB):
                            for hp in range(PAIRS):
                                mm = pe.matmul(bank[WIN * w:WIN * w + WIN, SC[par], hp * HD:(hp + 1) * HD],
                                               q_t[f, s % 2, hp, WIN * w:WIN * w + WIN],
                                               k_t[f, s % 2, hp, WIN * w:WIN * w + 2 * WIN],
                                               start=False, stop=True, skip_group_check=True)
                        mm.then_inc(S.scores, 1)

                    def turn_prob(s, g):
                        if g == 0:
                            pe.wait_ge(S.probs, 2 * (s + 1))
                        free_misc("prob", s, g)
                        for i in range(4):
                            mm = pe.transpose(bank[:, misc("prob", s, g), i * P:(i + 1) * P],
                                              prob[:, s % 2, 4 * g + i, :, :].rearrange("p a k -> p (a k)"), ident[:, :])
                        mm.then_inc(S.misc, 1)

                    def weigh_v(s, par):
                        if par == 0:
                            wait_misc(pe, turn["prob", s, 1])
                            wait_v_in(pe, s)
                            if s >= 2:
                                pe.wait_ge(S.look, 32 * (s - 1))
                        if s >= 1:
                            pe.wait_ge(S.av_out, 2 * s - 1 + par)
                        f = slice(64 * par, 64 * par + 64)
                        for w in range(WPB):
                            for hp in range(PAIRS):
                                mm = pe.matmul(bank[WIN * w:WIN * w + WIN, AV[par], hp * HD:(hp + 1) * HD],
                                               prob_t[f, s % 2, hp, WIN * w:WIN * w + WIN],
                                               v[f, s % 2, w, hp, :], start=True, stop=True)
                        mm.then_inc(S.av, 1)

                    def turn_att(s, g):
                        if g == 0:
                            pe.wait_ge(S.av_out, 2 * (s + 1))
                        free_misc("att", s, g)
                        for i in range(4):
                            mm = pe.transpose(bank[:, misc("att", s, g), i * P:(i + 1) * P],
                                              att[:, s % 2, 4 * g + i, :, :].rearrange("p a d -> p (a d)"), ident[:, :])
                        mm.then_inc(S.misc, 1)

                    def project_out(s):
                        if s == 0:
                            pe.wait_ge(S.weights, 64)
                        free_misc("out", s, 0)
                        wait_misc(pe, turn["att", s, 1])
                        o = bank[:, misc("out", s, 0), 0:BLK]
                        for hp in range(PAIRS):
                            mm = pe.matmul(o, w_o[:, hp, :], att_t[:, s % 2, hp, :], start=hp == 0, stop=hp == PAIRS - 1)
                        mm.then_inc(S.misc, 1)

                    def mean(i):
                        pe.wait_ge(S.f_shift, 2 * (i + 1))
                        if i < 2:
                            pe.wait_ge(S.v_out, 2 * SLOTS)
                        elif i == 2:
                            pe.wait_ge(S.shifted, 2 * SLOTS)
                        pe.matmul(bank[:, STAT[i], :], mean_w[:, :], f_x[:, i % 2, :], start=True, stop=True)\
                          .then_inc(S.f_mean, 1)

                    def variance(i):
                        pe.wait_ge(S.f_squared, i + 1)
                        pe.matmul(bank[:, STAT[i], :], mean_w[:, :], f_squares[:, i % 2, :], start=True, stop=True)\
                          .then_inc(S.f_var, 1)

                    def up(i):
                        pe.wait_ge(S.f_normed, i + 1)
                        for j in range(FB):
                            n = FB * i + j
                            m = FROWS[j]
                            if n == 0:
                                pe.wait_ge(S.f_ln, 2)
                            elif n == 1:
                                pe.wait_ge(S.av_out, 2 * SLOTS)
                            else:
                                pe.wait_ge(S.gated, n - 1)
                                pe.wait_ge(S.hidden, n - 1)
                            pe.matmul(bank[0:m, GATE[n % 2], :], w_1[:, FF + j * P:FF + j * P + m], f_norm[:, i, :],
                                      start=True, stop=True).then_inc(S.gate_mm, 1)
                            pe.matmul(bank[0:m, VALUE[n % 2], :], w_1[:, j * P:j * P + m], f_norm[:, i, :],
                                      start=True, stop=True).then_inc(S.value_mm, 1)

                    def down(i):
                        pe.wait_ge(S.hidden, FB * (i + 1))
                        if i == 0:
                            for n in (len(turn) - 2, len(turn) - 1):
                                wait_misc(pe, n)
                        if i >= 2:
                            pe.wait_ge(S.ff_out, i - 1)
                        for j in range(FB):
                            m = FROWS[j]
                            mm = pe.matmul(bank[:, MISC[i % 2], :], w_2[0:m, j, :], f_hid[0:m, i % 2, j, :],
                                           start=j == 0, stop=j == FB - 1)
                        mm.then_inc(S.down, 1)

                    for s in range(-2, SLOTS + 2):
                        for j in range(4):
                            if live(s):
                                turn_qk(s, j)
                            if live(s + 2):
                                project_qk(s + 2, j)
                        if live(s - 2):
                            turn_att(s - 2, 0)
                        if s == SLOTS - 1:
                            mean(0)
                            mean(1)
                        if live(s):
                            scores(s, 0)
                        if live(s - 2):
                            turn_att(s - 2, 1)
                        if live(s + 1):
                            project_v(s + 1, 0)
                        if live(s - 1):
                            turn_prob(s - 1, 0)
                            turn_prob(s - 1, 1)
                        if live(s):
                            scores(s, 1)
                        if live(s + 1):
                            project_v(s + 1, 1)
                        if s == SLOTS + 1:
                            up(0)
                        if s == SLOTS - 1:
                            variance(0)
                            variance(1)
                        if live(s - 1):
                            weigh_v(s - 1, 0)
                        if live(s - 2):
                            project_out(s - 2)
                        if live(s - 1):
                            weigh_v(s - 1, 1)
                        if s == SLOTS + 1:
                            variance(2)
                        if s == SLOTS:
                            mean(2)

                    mean(3)
                    up(1)
                    variance(3)
                    down(0)
                    down(1)
                    up(2)
                    up(3)
                    down(2)
                    down(3)

                @block.scalar
                def _(act):
                    def empty_qk(s, j):
                        if s >= 2 and j == 0:
                            act.wait_ge(S.rot_cos, s - 1)
                            act.wait_ge(S.rot_sin, 2 * (s - 1))
                        u = pj["qk", s, j]
                        act.wait_ge(S.proj, u + 1)
                        act.copy(qk[:, s % 2, j * CH:(j + 1) * CH], bank[:, PJ[u % 2], :]).then_inc(S.proj_out, 1)

                    def square_qk(s):
                        act.wait_ge(S.proj_out, 4 * (s + 1))
                        if s >= 1:
                            act.wait_ge(S.sumsq, s)
                            act.activation(sq[:, :], qk[:, s % 2, :], ACT.Square).then_inc(S.squared, 1)
                        else:
                            act.activation(sq[:, qk_halves[1]], qk[:, 0, qk_halves[1]], ACT.Square).then_inc(S.squared, 1)

                    def square_first_q(act):
                        act.wait_ge(S.proj_out, 2)
                        act.activation(sq[:, qk_halves[0]], qk[:, 0, qk_halves[0]], ACT.Square).then_inc(S.squared_first, 1)

                    def norm_qk(s):
                        if s == 0:
                            act.wait_ge(S.sumsq_first, 1)
                        act.wait_ge(S.sumsq, s + 1)
                        if s >= 2:
                            act.wait_ge(S.inv_norm, s - 1)
                        act.activation(rn[:, s % 2, :], ssq[:, s % 2, :], ACT.Sqrt).then_inc(S.norm, 1)

                    def empty_v(s, par):
                        if s >= 2 and par == 0:
                            wait_v_in(act, s - 2)
                        u = pj["v", s, par]
                        act.wait_ge(S.proj, u + 1)
                        act.copy(v_tok[:, s % 2, par, :], bank[:, PJ[u % 2], :]).then_inc(S.v_out, 1)

                    def look_back(s):
                        act.wait_ge(S.scores, 2 * (s - 1))
                        act.copy(k_t[:, s % 2, :, 0:WIN], k_t[:, s % 2, :, BLK:BLK + WIN]).then_inc(S.lookback, 1)

                    def empty_turned(s, g):
                        if s >= 2 and g == 0:
                            act.wait_ge(S.scores, 2 * (s - 1))
                        act.wait_ge(S.misc, turn["turn", s, g] + 1)
                        src = bank[:, misc("turn", s, g), :].rearrange("p (h t) -> p h t", t=BLK)
                        if g < 2:
                            dst = q_t[:, s % 2, 4 * g:4 * g + 4, :]
                        else:
                            if s >= 2:
                                act.wait_ge(S.lookback, s - 1)
                            dst = k_t[:, s % 2, 4 * g - 8:4 * g - 4, WIN:WIN + BLK]
                        act.copy(dst, src).then_inc(S.misc_out, 1)

                    def empty_pairs(kind, dst, s, g):
                        act.wait_ge(S.misc, turn[kind, s, g] + 1)
                        act.copy(dst[:, s % 2, 4 * g:4 * g + 4, :].rearrange("p h t -> p (h t)"),
                                 bank[:, misc(kind, s, g), :]).then_inc(S.misc_out, 1)

                    def empty_att(s, g):
                        if s >= 2 and g == 0:
                            act.wait_ge(S.misc, turn["out", s - 2, 0] + 1)
                        empty_pairs("att", att_t, s, g)

                    def empty_prob(s, g):
                        if s >= 2 and g == 0:
                            act.wait_ge(S.av, 2 * (s - 1))
                        empty_pairs("prob", prob_t, s, g)

                    def exponent(s):
                        for par in range(2):
                            act.wait_ge(S.shifted, 2 * s + par + 1)
                            act.activation(prob[:, s % 2, :, par, :], prob[:, s % 2, :, par, :], ACT.Exp).then_inc(S.probs, 1)

                    def square(i):
                        act.wait_ge(S.f_centered, i + 1)
                        if i == 0:
                            act.wait_ge(S.sumsq, SLOTS)
                        if i >= 2:
                            act.wait_ge(S.f_var, i - 1)
                        act.activation(f_squares[:, i % 2, :], f_norm[:, i, :], ACT.Square).then_inc(S.f_squared, 1)

                    def log_variance(i):
                        act.wait_ge(S.f_var, i + 1)
                        if i == 0:
                            act.wait_ge(S.rot_cos, SLOTS)
                            act.wait_ge(S.rot_sin, 2 * SLOTS)
                        act.activation(f_rstd[:, i, :], bank[:, STAT[i], :], ACT.Ln, bias=eps[:, :]).then_inc(S.f_ln, 1)

                    def inverse_dev(i):
                        act.wait_ge(S.f_ln, i + 1)
                        act.activation(f_rstd[:, i, :], f_rstd[:, i, :], ACT.Exp, scale=-0.5).then_inc(S.f_rstd, 1)

                    def gate(i):
                        if i == 0:
                            wait_rotated(act, SLOTS - 1)
                            act.wait_ge(S.weights, 64)
                        for j in range(FB):
                            n = FB * i + j
                            m = FROWS[j]
                            act.wait_ge(S.gate_mm, n + 1)
                            if n >= 2:
                                act.wait_ge(S.hidden, n - 1)
                            act.activation(f_gate[0:m, n % 2, :], bank[0:m, GATE[n % 2], :], ACT.Gelu,
                                           bias=lvec[0:m, 6 + j:7 + j]).then_inc(S.gated, 1)

                    for s in range(-2, SLOTS + 2):
                        if live(s) and s >= 2:
                            look_back(s)
                        for j in range(4):
                            if live(s):
                                empty_turned(s, j)
                            if live(s + 2):
                                empty_qk(s + 2, j)
                            if s == -2 and j == 2:
                                square_first_q(act)
                        if live(s - 2):
                            empty_att(s - 2, 0)
                        if s == SLOTS - 1:
                            square(0)
                            square(1)
                        if live(s - 2):
                            empty_att(s - 2, 1)
                        if live(s + 1):
                            empty_v(s + 1, 0)
                        if live(s - 1):
                            empty_prob(s - 1, 0)
                            empty_prob(s - 1, 1)
                        if live(s + 2):
                            square_qk(s + 2)
                        if live(s + 1):
                            empty_v(s + 1, 1)
                        if s == SLOTS + 1:
                            gate(0)
                        if live(s):
                            exponent(s)
                        if live(s + 2):
                            norm_qk(s + 2)
                        if s == SLOTS - 1:
                            log_variance(0)
                            log_variance(1)
                            inverse_dev(0)
                            inverse_dev(1)
                        if s == SLOTS:
                            square(2)

                    square(3)
                    gate(1)
                    log_variance(2)
                    log_variance(3)
                    inverse_dev(2)
                    inverse_dev(3)
                    gate(2)
                    act.wait_ge(S.next_w, 16)
                    for j in range(3):
                        split_high(act, j, S.w_high)
                    gate(3)
                    for j in range(3, 6):
                        split_high(act, j, S.w_high)

                @block.vector
                def _(dve):
                    def stage(s):
                        lo = PAD + (s // 2) * BLK
                        if s >= XS:
                            dve.wait_ge(S.proj, pj["v", s - XS, 1] + 1)
                        halves = ((slice(0, 64), 0), (slice(64, P), 1))
                        for f, back in halves:
                            dve.tensor_copy(x_high[f, s % XS, :], h_in[f, s % 2, lo - back:lo - back + BLK]).then_inc(S.staged_high, 1)
                        dve.wait_ge(S.staged_high, 2 * (s + 1))
                        for f, back in halves:
                            dve.tensor_tensor(x_low[f, s % XS, :], h_in[f, s % 2, lo - back:lo - back + BLK],
                                              x_high[f, s % XS, :].bitcast(F32), ALU.subtract).then_inc(S.staged, 1)

                    def sum_squares(s):
                        if s == 0:
                            dve.wait_ge(S.squared_first, 1)
                            dve.tensor_reduce(ssq[:, 0, 0:HEADS], sq[:, qk_halves[0]].rearrange("p (h d) -> p h d", d=HD),
                                              AX.X, ALU.add).then_inc(S.sumsq_first, 1)
                            dve.wait_ge(S.squared, 1)
                            dve.tensor_reduce(ssq[:, 0, HEADS:], sq[:, qk_halves[1]].rearrange("p (h d) -> p h d", d=HD),
                                              AX.X, ALU.add).then_inc(S.sumsq, 1)
                            return
                        dve.wait_ge(S.squared, s + 1)
                        if s >= 2:
                            dve.wait_ge(S.norm, s - 1)
                        dve.tensor_reduce(ssq[:, s % 2, :], sq[:, :].rearrange("p (h d) -> p h d", d=HD), AX.X, ALU.add)\
                           .then_inc(S.sumsq, 1)

                    def normalise(s):
                        r = rn[:, s % 2, :]
                        dve.wait_ge(S.norm, s + 1)
                        dve.tensor_scalar(r, r, 1e-12, None, ALU.max).then_inc(S.clamped, 1)
                        dve.wait_ge(S.clamped, s + 1)
                        dve.reciprocal(r, r).then_inc(S.inv_norm, 1)
                        dve.wait_ge(S.inv_norm, s + 1)
                        heads = qk[:, s % 2, :].rearrange("p (h d) -> p h d", d=HD)
                        dve.tensor_tensor(heads, heads, r.unsqueeze(2).to_broadcast([P, 2 * HEADS, HD]), ALU.mult)\
                           .then_inc(S.normed, 1)
                        dve.wait_ge(S.normed, s + 1)
                        if s >= 2:
                            dve.wait_ge(S.misc, turn["turn", s - 2, 3] + 1)
                        dve.tensor_tensor(qr[:, s % 2, :].rearrange("p (a h d) -> p a h d", a=2, h=HEADS),
                                          qk[:, s % 2, :].rearrange("p (a h d) -> p a h d", a=2, h=HEADS),
                                          cos[:, s // 2, :].rearrange("p (a d) -> p a d", a=2).unsqueeze(2)
                                          .to_broadcast([P, 2, HEADS, HD]), ALU.mult).then_inc(S.rot_cos, 1)
                        if s == 0:
                            src = qk[:, 0, :].rearrange("p (a h i d) -> p a h i d", a=2, h=HEADS, i=2)
                            dst = t_sin[:, :].rearrange("p (a h i d) -> p a h i d", a=2, h=HEADS, i=2)
                            tab = sin[:, 0, :].rearrange("p (a i d) -> p a i d", a=2, i=2)
                            dve.tensor_tensor(dst[:, :, :, 1, :], src[:, :, :, 0, :],
                                              tab[:, :, 1, :].unsqueeze(2).to_broadcast([P, 2, HEADS, 32]),
                                              ALU.mult).then_inc(S.rot_sin, 1)
                            dve.wait_ge(S.rot_cos, 1)
                            dve.wait_ge(S.rot_sin, 2)
                            for half in qk_halves:
                                dve.tensor_tensor(qr[:, 0, half], qr[:, 0, half], t_sin[:, half], ALU.add)\
                                   .then_inc(S.rotated_first, 1)

                    def shift_scores(s):
                        if s >= 2:
                            dve.wait_ge(S.misc, turn["prob", s - 2, 1] + 1)
                            dve.wait_ge(S.rowsum, s - 1)
                        if s >= 1:
                            dve.wait_ge(S.shifted, 2 * s)
                        for par in range(2):
                            dve.wait_ge(S.scores, 2 * s + par + 1)
                            dve.tensor_reduce(row_max[:, par, :], bank[:, SC[par], :].rearrange("p (h k) -> p h k", k=HD),
                                              AX.X, ALU.max).then_inc(S.rowmax, 1)
                            dve.wait_ge(S.rowmax, 2 * s + par + 1)
                            dve.tensor_tensor(prob[:, s % 2, :, par, :],
                                              bank[:, SC[par], :].rearrange("p (h k) -> p h k", k=HD),
                                              row_max[:, par, :].unsqueeze(2).to_broadcast([P, PAIRS, HD]),
                                              ALU.subtract).then_inc(S.shifted, 1)

                    def sum_probs(s):
                        r = row_sum[:, s % 2, :]
                        dve.wait_ge(S.probs, 2 * (s + 1))
                        if s >= 2:
                            dve.wait_ge(S.av_out, 2 * (s - 1))
                        dve.tensor_reduce(r, prob[:, s % 2, :, :, :].rearrange("p h a k -> p (h a) k"), AX.X, ALU.add)\
                           .then_inc(S.rowsum, 1)
                        dve.wait_ge(S.rowsum, s + 1)
                        dve.reciprocal(r, r).then_inc(S.inv_sum, 1)

                    def norm_att(s, par):
                        if par == 0:
                            dve.wait_ge(S.inv_sum, s + 1)
                            if s >= 2:
                                dve.wait_ge(S.misc, turn["att", s - 2, 1] + 1)
                        dve.wait_ge(S.av, 2 * s + par + 1)
                        r = row_sum[:, s % 2, :].rearrange("p (h a) -> p h a", a=2)[:, :, par:par + 1]
                        dve.tensor_tensor(att[:, s % 2, :, par, :],
                                          bank[:, AV[par], :].rearrange("p (h d) -> p h d", d=HD),
                                          r.to_broadcast([P, PAIRS, HD]), ALU.mult).then_inc(S.av_out, 1)

                    def add_residual(s):
                        dve.wait_ge(S.misc, turn["out", s, 0] + 1)
                        dve.tensor_tensor(tokens(h_mid, s), tokens(h_in, s), bank[:, misc("out", s, 0), 0:BLK],
                                          ALU.add).then_inc(S.out_done, 1)

                    def shift_tokens(i):
                        c = ORDER[i]
                        last = (6, 7, SLOTS - 2, SLOTS - 1)[i]
                        wait_misc(dve, turn["out", last, 0])
                        if i == 0:
                            dve.wait_ge(S.sumsq, SLOTS)
                        if i >= 2:
                            dve.wait_ge(S.f_centered, i - 1)
                        lo = PAD + (c % 2) * CH
                        for f, back in ((slice(0, 64), 0), (slice(64, P), 1)):
                            dve.tensor_copy(f_x[f, i % 2, :], h_mid[f, c // 2, lo - back:lo - back + CH]).then_inc(S.f_shift, 1)

                    def center(i):
                        if i == 0:
                            dve.wait_ge(S.rot_cos, SLOTS)
                            dve.wait_ge(S.rot_sin, 2 * SLOTS)
                        dve.wait_ge(S.f_shift, 2 * (i + 1))
                        dve.wait_ge(S.f_mean, i + 1)
                        dve.tensor_tensor(f_norm[:, i, :], f_x[:, i % 2, :], bank[:, STAT[i], :], ALU.subtract)\
                           .then_inc(S.f_centered, 1)

                    def norm(i):
                        if i == 0:
                            dve.wait_ge(S.weights, 64)
                        dve.wait_ge(S.f_squared, i + 1)
                        dve.wait_ge(S.f_rstd, i + 1)
                        dve.scalar_tensor_tensor(out=f_norm[:, i, :], in0=f_norm[:, i, :], scalar=lvec[:, 0:1],
                                                 in1=f_rstd[:, i, :], op0=ALU.mult, op1=ALU.mult).then_inc(S.f_scaled, 1)
                        dve.wait_ge(S.f_scaled, i + 1)
                        dve.tensor_scalar(f_norm[:, i, :], f_norm[:, i, :], lvec[:, 1:2], None, ALU.add).then_inc(S.f_normed, 1)

                    def hidden(i):
                        if i == 0:
                            dve.wait_ge(S.misc, turn["turn", SLOTS - 1, 3] + 1)
                        for j in range(FB):
                            n = FB * i + j
                            m = FROWS[j]
                            if i >= 2 and j == 0:
                                dve.wait_ge(S.down, i - 1)
                            dve.wait_ge(S.value_mm, n + 1)
                            dve.wait_ge(S.gated, n + 1)
                            dve.scalar_tensor_tensor(out=f_hid[0:m, i % 2, j, :], in0=bank[0:m, VALUE[n % 2], :],
                                                     scalar=lvec[0:m, 3 + j:4 + j], in1=f_gate[0:m, n % 2, :],
                                                     op0=ALU.add, op1=ALU.mult).then_inc(S.hidden, 1)

                    def finish(i):
                        c = ORDER[i]
                        dve.wait_ge(S.down, i + 1)
                        dve.scalar_tensor_tensor(out=padded(h_in, c), in0=bank[:, MISC[i % 2], :], scalar=lvec[:, 2:3],
                                                 in1=padded(h_mid, c), op0=ALU.add, op1=ALU.add).then_inc(S.ff_out, 1)

                    stage(0)
                    stage(1)
                    stage(2)
                    for s in range(-2, SLOTS + 2):
                        if s >= 0 and live(s + 3):
                            stage(s + 3)
                        if live(s - 1):
                            sum_probs(s - 1)
                        if s == SLOTS - 1:
                            shift_tokens(0)
                            shift_tokens(1)
                            center(0)
                            center(1)
                        if live(s + 1):
                            normalise(s + 1)
                        if live(s):
                            shift_scores(s)
                        if live(s + 2):
                            sum_squares(s + 2)
                        if live(s - 1):
                            norm_att(s - 1, 0)
                        if s == SLOTS + 1:
                            hidden(0)
                        if live(s - 2):
                            add_residual(s - 2)
                        if live(s - 1):
                            norm_att(s - 1, 1)
                        if s == SLOTS - 1:
                            norm(0)
                            norm(1)
                        if s == SLOTS:
                            shift_tokens(2)
                            center(2)
                        if s == SLOTS + 1:
                            shift_tokens(3)

                    center(3)
                    hidden(1)
                    finish(0)
                    norm(2)
                    norm(3)
                    finish(1)
                    hidden(2)
                    dve.wait_ge(S.next_w, 16)
                    for j in range(3):
                        split_low(dve, j, S.w_high, S.w_low)
                    hidden(3)
                    finish(2)
                    for j in range(3, 6):
                        split_low(dve, j, S.w_high, S.w_low)
                    finish(3)
                    dve.wait_ge(S.ff_out, NCH)
                    dve.wait_ge(S.w_low, 6)
            nc.all_engine_barrier(sems_to_clear=span)


def full_attention(nc, A, sb, sem, bank, ident, h_in, padded, x_chunk, mod):
    QB = N // P
    UNITS = B * QB
    UPC = CH // P
    SCALE = HD ** -0.5
    with ExitStack() as ctx:
        def buf(name, shape, dt=F32):
            return sb(f"fa_{name}", shape, dt, ctx=ctx)

        anti = buf("anti", [P, P])
        w_out = buf("w_out", [P, P])
        w = buf("w", [P, 3, P])
        w_high = buf("w_high", [P, 4, 2, HD], F32R)
        w_low = buf("w_low", [P, 4, 2, HD], F32R)
        h_high = buf("h_high", [P, B, N], F32R)
        h_low = buf("h_low", [P, B, N], F32R)
        rel = buf("rel", [P, 2, 2 * P])
        q_high = buf("q_high", [P, 2, B, N], F32R)
        q_low = buf("q_low", [P, 2, B, N], F32R)
        k_both = buf("k_both", [P, 2, B, N], F32R)
        v = buf("v", [P, B, QB, P])
        neg_max = buf("neg_max", [P, 2, 2, 2])
        row_sum = buf("row_sum", [P, 2, 2])
        inv_sum = buf("inv_sum", [P, 2, 2])
        prob = buf("prob", [P, 2, 2, N])
        prob_t = buf("prob_t", [P, 2, 2, QB, P])
        att_t = buf("att_t", [P, B, N])

        s_load = sem("s_fa_load")
        s_high = sem("s_fa_h_high")
        s_low = sem("s_fa_h_low")

        s_w_high = sem("s_fa_first_w_high")
        s_w_low = sem("s_fa_first_w_low")

        def h_part(t, c):
            return t[:, c // 2, (c % 2) * CH:(c % 2 + 1) * CH]

        def twice():
            return w[:, 0:2, :].rearrange("p t (h d) -> p (t h) d", h=2).unsqueeze(2).to_broadcast([P, 4, 2, HD])

        def split_high(act, done):
            act.copy(w_high[:, :, :, :], twice()).then_inc(done, 1)

        def split_low(dve, high_done, done):
            dve.wait_ge(high_done, 1)
            dve.tensor_tensor(w_low[:, :, :, :], twice(), w_high[:, :, :, :].bitcast(F32), ALU.subtract).then_inc(done, 1)

        with nc.Block(no_gpsimd_drain=True) as block:
            @block.sync
            def _(sp):
                sp.dma_start(anti[:, :], A["anti"]).then_inc(s_load, 16)
                sp.dma_start(w[:, :, :], A["fa_w"][0]).then_inc(s_load, 16)
                sp.wait_ge(s_load, 32)

            @block.scalar
            def _(act):
                for c in range(NCH):
                    act.copy(h_part(h_high, c), padded(h_in, c)).then_inc(s_high, 1)
                act.wait_ge(s_load, 32)
                split_high(act, s_w_high)

            @block.vector
            def _(dve):
                for c in range(NCH):
                    dve.wait_ge(s_high, c + 1)
                    dve.tensor_tensor(h_part(h_low, c), padded(h_in, c), h_part(h_high, c).bitcast(F32),
                                      ALU.subtract).then_inc(s_low, 1)
                dve.wait_ge(s_low, NCH)
                dve.wait_ge(s_load, 32)
                split_low(dve, s_w_high, s_w_low)
                dve.wait_ge(s_w_low, 1)

        names = ("next w_out_in rel_in rel8 w_high w_low proj high low v_out scores rowmax negmax probs inv_sum scaled turned turned_a turned_v "
                 "av att_out y").split()
        first = {n: sem(f"s_fa_{n}", ctx) for n in names}
        S = type("S", (), first)
        numbers = [s.num for s in first.values()]
        span = range(min(numbers), max(numbers) + 1)
        PROJ = 4 * B * 2
        V_USES = NCH

        TURN = (4, 5, 7)
        AVB = 6
        uses, on_a, on_v = {}, 0, 0
        for u in range(UNITS + 3):
            step = [("prob", u, i) for i in range(4)] if u < UNITS else []
            if u % UPC == 2 and u > UPC:
                step = step + [("out", u // UPC - 1, 0)]
            for use in step:
                if use[0] == "prob" and use[2] != 3:
                    on_a += 1
                    uses[use] = (len(uses), "a", on_a)
                else:
                    on_v += 1
                    uses[use] = (len(uses), "v", on_v)
        by_number = {n: (eng, count) for n, eng, count in uses.values()}

        def turn_bank(use):
            return TURN[uses[use][0] % len(TURN)]

        def wait_emptied(eng, n):
            who, count = by_number[n]
            eng.wait_ge(S.turned_a if who == "a" else S.turned_v, count)

        def empty_turned(copy, eng, u, i):
            use = ("prob", u, i)
            eng.wait_ge(S.turned, 4 * u + i + 1)
            if u >= 2:
                eng.wait_ge(S.av, u - 1)
            copy(prob_t[:, u % 2, i // 2, 4 * (i % 2):4 * (i % 2) + 4, :].rearrange("p k q -> p (k q)"),
                 bank[:, turn_bank(use), :]).then_inc(S.turned_a if uses[use][1] == "a" else S.turned_v, 1)

        with nc.Fori(0, PAIRS) as pair:
            with nc.Block(no_gpsimd_drain=True) as block:
                @block.sync
                def _(sp):
                    sp.dma_start(rel[:, :, :], A["fa_rel"][pair]).then_inc(S.rel_in, 16)
                    sp.dma_start(w_out[:, :], A["fa_wout"][pair]).then_inc(S.w_out_in, 16)
                    sp.wait_ge(S.proj, PROJ + V_USES)
                    sp.dma_start(w[:, :, :], A["fa_w"][pair + 1]).then_inc(S.next, 16)
                    sp.wait_ge(S.next, 16)
                    sp.wait_ge(S.rel_in, 16)
                    sp.wait_ge(S.w_out_in, 16)

                @block.tensor
                def _(pe):
                    for n in range(PROJ):
                        b, t, c = n // 8, n % 8 // 2, 2 * (n // 8) + n % 2
                        if n >= 8:
                            pe.wait_ge(S.low, n - 7)
                        o = bank[:, n % 8, :]
                        high = w_high[:, t, :, :].rearrange("p a d -> p (a d)")
                        low = w_low[:, t, :, :].rearrange("p a d -> p (a d)")
                        pe.matmul(o, high, h_part(h_high, c), start=True, stop=False)
                        pe.matmul(o, high, h_part(h_low, c), start=False, stop=False)
                        pe.matmul(o, low, h_part(h_high, c), start=False, stop=True).then_inc(S.proj, 1)
                    def project_v():
                        for c in range(V_USES):
                            pe.wait_ge(S.low, PROJ - 3 + c)
                            for t in range(4):
                                lo = PAD + ((c % 2) * 4 + t) * P
                                mm = pe.matmul(bank[:, 4 + c, t * P:(t + 1) * P], h_in[:, c // 2, lo:lo + P], w[:, 2, :],
                                               start=True, stop=True)
                            mm.then_inc(S.proj, 1)

                    def scores(u, par):
                        b, qb = u // QB, u % QB
                        if u >= 1:
                            pe.wait_ge(S.probs, 2 * (u - 1) + par + 1)
                        for half in range(2):
                            near = qb >= 6 and half == 0
                            o = bank[:, 2 * par + half, :]
                            k = k_both[:, par, b, half * CH:(half + 1) * CH]
                            pe.matmul(o, q_high[:, par, b, qb * P:(qb + 1) * P], k, start=True, stop=False)
                            mm = pe.matmul(o, q_low[:, par, b, qb * P:(qb + 1) * P], k, start=False, stop=not near)
                            if near:
                                if u == 6:
                                    pe.wait_ge(S.rel8, 4)
                                cols = slice(P, 2 * P) if qb == 6 else slice(0, 2 * P)
                                mm = pe.matmul(o[:, 0:P * (qb - 5)], anti[:, :], rel[:, par, cols], start=False, stop=True)
                        mm.then_inc(S.scores, 1)

                    def turn(u):
                        for i in range(4):
                            use = ("prob", u, i)
                            if i % 2 == 0:
                                pe.wait_ge(S.scaled, 2 * u + i // 2 + 1)
                            if uses[use][0] >= len(TURN):
                                wait_emptied(pe, uses[use][0] - len(TURN))
                            for j in range(4):
                                at = 4 * (i % 2) + j
                                mm = pe.transpose(bank[:, turn_bank(use), j * P:(j + 1) * P],
                                                  prob[:, u % 2, i // 2, at * P:(at + 1) * P], ident[:, :])
                            mm.then_inc(S.turned, 1)

                    def weigh_v(u):
                        wait_emptied(pe, uses["prob", u, 3][0])
                        wait_emptied(pe, uses["prob", u, 2][0])
                        c, i = u // UPC, u % UPC
                        if i == 0 and c >= 1:
                            pe.wait_ge(S.att_out, c)
                        for kb in range(QB):
                            for par in range(2):
                                mm = pe.matmul(bank[HD * par:HD * par + HD, AVB, i * P:(i + 1) * P],
                                               v[:, u // QB, kb, HD * par:HD * par + HD], prob_t[:, u % 2, par, kb, :],
                                               start=kb == 0, stop=kb == QB - 1)
                        mm.then_inc(S.av, 1)

                    def project_out(c):
                        use = ("out", c, 0)
                        pe.wait_ge(S.att_out, c + 1)
                        wait_emptied(pe, uses[use][0] - len(TURN))
                        if c == 0:
                            pe.wait_ge(S.w_out_in, 16)
                        pe.matmul(bank[:, turn_bank(use), :], w_out[:, :], h_part(att_t, c), start=True, stop=True)\
                          .then_inc(S.y, 1)

                    pe.wait_ge(S.low, PROJ)
                    scores(0, 0)
                    scores(0, 1)
                    project_v()
                    for u in range(UNITS + 3):
                        for par in range(2):
                            if u + 1 < UNITS:
                                scores(u + 1, par)
                        if u == 0:
                            pe.wait_ge(S.v_out, V_USES)
                        if u < UNITS:
                            turn(u)
                        if ("out", u // UPC - 1, 0) in uses and u % UPC == 2:
                            project_out(u // UPC - 1)
                        if 1 <= u < UNITS + 1:
                            weigh_v(u - 1)

                @block.scalar
                def _(act):
                    for n in range(PROJ):
                        t, c = n % 8 // 2, 2 * (n // 8) + n % 2
                        dst = h_part((q_high if t < 2 else k_both)[:, t % 2, :, :], c)
                        act.wait_ge(S.proj, n + 1)
                        act.copy(dst, bank[:, n % 8, :]).then_inc(S.high, 1)
                    def empty_v(c):
                        act.wait_ge(S.proj, PROJ + c + 1)
                        act.copy(v[:, c // 2, 4 * (c % 2):4 * (c % 2) + 4, :].rearrange("p t d -> p (t d)"), bank[:, 4 + c, :])\
                           .then_inc(S.v_out, 1)

                    def exponent(u, par):
                        if u >= UNITS:
                            return
                        act.wait_ge(S.negmax, 2 * u + par + 1)
                        if u >= 2:
                            act.wait_ge(S.turned, 4 * (u - 2) + 2 * par + 2)
                            act.wait_ge(S.inv_sum, 2 * (u - 2) + par + 1)
                        act.activation(prob[:, u % 2, par, :], bank[:, 2 * par:2 * par + 2, :].rearrange("p a n -> p (a n)"),
                                       ACT.Exp, bias=neg_max[:, u % 2, par, 1:2], scale=SCALE,
                                       accum_out=row_sum[:, u % 2, par:par + 1]).then_inc(S.probs, 1)

                    def empty_att(c):
                        act.wait_ge(S.av, UPC * (c + 1))
                        if c >= 1:
                            act.wait_ge(S.y, c)
                        act.copy(h_part(att_t, c), bank[:, AVB, :]).then_inc(S.att_out, 1)

                    exponent(0, 0)
                    empty_v(0)
                    exponent(0, 1)
                    for c in range(1, V_USES):
                        empty_v(c)
                    for u in range(UNITS + 2):
                        if u < UNITS:
                            empty_turned(act.copy, act, u, 0)
                            empty_turned(act.copy, act, u, 1)
                        exponent(u + 1, 0)
                        if u < UNITS:
                            empty_turned(act.copy, act, u, 2)
                        exponent(u + 1, 1)
                        if u >= 1 and u % UPC == 0:
                            empty_att(u // UPC - 1)
                        if u == UNITS - 2:
                            act.wait_ge(S.next, 16)
                            split_high(act, S.w_high)

                @block.vector
                def _(dve):
                    for n in range(PROJ):
                        t, c = n % 8 // 2, 2 * (n // 8) + n % 2
                        dve.wait_ge(S.high, n + 1)
                        if t < 2:
                            high, low = h_part(q_high[:, t, :, :], c), h_part(q_low[:, t, :, :], c)
                            dve.tensor_tensor(low, bank[:, n % 8, :], high.bitcast(F32), ALU.subtract).then_inc(S.low, 1)
                        else:
                            both = h_part(k_both[HD:P, t - 2, :, :], c)
                            dve.tensor_tensor(both, bank[HD:P, n % 8, :], both.bitcast(F32), ALU.subtract).then_inc(S.low, 1)
                    dve.wait_ge(S.rel_in, 16)
                    for par in range(2):
                        dve.tensor_scalar(rel[:, par, 0:2 * P - 1], rel[:, par, 0:2 * P - 1], rel[:, par, 2 * P - 1:2 * P],
                                          1.0 / SCALE, ALU.subtract, ALU.mult).then_inc(S.rel8, 1)
                    dve.wait_ge(S.rel8, 2)
                    for par in range(2):
                        dve.memset(rel[:, par, 2 * P - 1:2 * P], 0.0).then_inc(S.rel8, 1)

                    def maximum(u):
                        for par in range(2):
                            m = neg_max[:, u % 2, par, :]
                            dve.wait_ge(S.scores, 2 * u + par + 1)
                            if u >= 2:
                                dve.wait_ge(S.probs, 2 * (u - 2) + par + 1)
                            dve.tensor_reduce(m[:, 0:1], bank[:, 2 * par:2 * par + 2, :].rearrange("p a n -> p (a n)"),
                                              AX.X, ALU.max).then_inc(S.rowmax, 1)
                            dve.wait_ge(S.rowmax, 2 * u + par + 1)
                            dve.tensor_scalar(m[:, 1:2], m[:, 0:1], -SCALE, None, ALU.mult).then_inc(S.negmax, 1)

                    def scale_probs(u):
                        for par in range(2):
                            r = inv_sum[:, u % 2, par:par + 1]
                            dve.wait_ge(S.probs, 2 * u + par + 1)
                            if u >= 2:
                                dve.wait_ge(S.scaled, 2 * (u - 2) + par + 1)
                            dve.reciprocal(r, row_sum[:, u % 2, par:par + 1]).then_inc(S.inv_sum, 1)
                            dve.wait_ge(S.inv_sum, 2 * u + par + 1)
                            dve.tensor_scalar(prob[:, u % 2, par, :], prob[:, u % 2, par, :], r, None, ALU.mult)\
                               .then_inc(S.scaled, 1)

                    def add(c):
                        dve.wait_ge(S.y, c + 1)
                        dve.scalar_tensor_tensor(out=x_chunk(c), in0=bank[:, turn_bank(("out", c, 0)), :],
                                                 scalar=mod[:, 1, 2, c // 2:c // 2 + 1], in1=x_chunk(c),
                                                 op0=ALU.mult, op1=ALU.add).then_inc(S.turned_v, 1)

                    maximum(0)
                    scale_probs(0)
                    for u in range(UNITS + 3):
                        if u + 1 < UNITS:
                            maximum(u + 1)
                        if u < UNITS:
                            empty_turned(dve.tensor_copy, dve, u, 3)
                        if ("out", u // UPC - 1, 0) in uses and u % UPC == 2:
                            add(u // UPC - 1)
                        if u + 1 < UNITS:
                            scale_probs(u + 1)
                        if u == UNITS - 1:
                            dve.wait_ge(S.next, 16)
                            split_low(dve, S.w_high, S.w_low)
                    dve.wait_ge(S.rel8, 4)
                    dve.wait_ge(S.turned_v, on_v)
                    dve.wait_ge(S.w_low, 1)
            nc.all_engine_barrier(sems_to_clear=span)


def experts(nc, A, sb, sem, bank, ident, h_in, x_main, mod, out):
    with ExitStack() as ctx:
        def buf(name, shape, dt=F32):
            return sb(f"ex_{name}", shape, dt, ctx=ctx)

        gate_w = buf("gate_w", [P, EXPERTS])
        b2 = buf("b2", [EXPERTS, P])
        iota = buf("iota", [P, EXPERTS])
        logits = buf("logits", [P, TB, EXPERTS])
        top = buf("top", [P, TB, 8])
        top_i = buf("top_i", [P, TB, 8], U32)
        top_f = buf("top_f", [P, TB, 8])
        pick = buf("pick", [P, 2, TB, EXPERTS])
        wt = buf("wt", [P, 4, TB])
        cw = buf("cw", [P, TB, EXPERTS])
        cw_t = buf("cw_t", [EXPERTS, TB, P])
        gb_diag = buf("gb_diag", [P, B, P])
        gb_all = buf("gb_all", [P, B, P])
        ones = buf("ones", [P, P])
        acc = buf("acc", [P, TB, P])
        w1 = buf("w1", [P, 2, EF])
        w1_high = buf("w1_high", [P, 2, EF], F32R)
        w1_low = buf("w1_low", [P, 2, EF], F32R)
        h_high = buf("h_high", [P, B, N], F32R)
        h_low = buf("h_low", [P, B, N], F32R)
        w2 = buf("w2", [P, 2, EFB, P])
        b1 = buf("b1", [P, 2, EFB])
        cw_e = buf("cw_e", [P, 2, TB])
        hid = buf("hid", [P, 2, EFB, CH])
        y = buf("y", [P, TB, P])

        s_in = sem("s_ex_in")
        s_w = sem("s_ex_first")
        s_ones = sem("s_ex_ones")
        s_lg = sem("s_ex_logits")
        s_lo = sem("s_ex_logits_out")
        s_top = sem("s_ex_top")
        s_idx = sem("s_ex_index")
        s_idf = sem("s_ex_index_f")
        s_diff = sem("s_ex_diff")
        s_exp = sem("s_ex_exp")
        s_wt = sem("s_ex_wt")
        s_cw = sem("s_ex_cw")
        s_ct = sem("s_ex_cwt")
        s_cto = sem("s_ex_cwt_out")
        s_b2 = sem("s_ex_b2")
        s_b2o = sem("s_ex_b2_out")
        s_gb = sem("s_ex_gb")
        s_gbm = sem("s_ex_gb_mm")
        s_gbo = sem("s_ex_gb_out")
        s_high = sem("s_ex_first_high")
        s_low = sem("s_ex_first_low")

        def split_high(act, k, done):
            act.copy(w1_high[:, k, :], w1[:, k, :]).then_inc(done, 1)

        def split_low(pool, k, done):
            pool.tensor_tensor(w1_low[:, k, :], w1[:, k, :], w1_high[:, k, :].bitcast(F32), ALU.subtract).then_inc(done, 1)

        def h_block(t):
            lo = PAD + (t % (TB // B)) * P
            return h_in[:, t // (TB // B), lo:lo + P]

        with nc.Block(no_gpsimd_drain=True) as block:
            @block.sync
            def _(sp):
                sp.dma_start(gate_w[:, :], A["gate_w"]).then_inc(s_in, 16)
                sp.dma_start(b2[:, :], A["ex_b2"]).then_inc(s_in, 16)
                sp.dma_start(iota[:, :], A["iota"]).then_inc(s_in, 16)
                sp.dma_start(w1[:, 0, :], A["ex_w1"][0]).then_inc(s_w, 16)
                sp.dma_start(w2[:, 0, :, :], A["ex_w2"][0]).then_inc(s_w, 16)
                sp.dma_start(b1[:, 0, :], A["ex_b1"][0]).then_inc(s_w, 16)
                sp.wait_ge(s_in, 48)
                sp.wait_ge(s_w, 48)

            @block.gpsimd
            def _(pool):
                pool.memset(ones[:, :], 1.0).then_inc(s_ones, 1)
                pool.wait_ge(s_ones, 1)
                for b in range(B):
                    pool.wait_ge(s_high, b + 1)
                    pool.tensor_tensor(h_low[:, b, :], h_in[:, b, PAD:PAD + N], h_high[:, b, :].bitcast(F32), ALU.subtract)\
                        .then_inc(s_low, 1)
                pool.wait_ge(s_high, 3)
                split_low(pool, 0, s_low)
                pool.wait_ge(s_low, 3)

            @block.tensor
            def _(pe):
                pe.wait_ge(s_in, 48)
                for t in range(TB):
                    mm = pe.matmul(bank[:, 0, t * EXPERTS:(t + 1) * EXPERTS], h_block(t), gate_w[:, :], start=True, stop=True)
                mm.then_inc(s_lg, 1)
                pe.wait_ge(s_ones, 1)
                pe.wait_ge(s_gb, 2)
                for b in range(B):
                    mm = pe.matmul(bank[:, 1, b * P:(b + 1) * P], ones[:, :], gb_diag[:, b, :], start=True, stop=True)
                mm.then_inc(s_gbm, 1)
                pe.wait_ge(s_cw, 3)
                for g in range(4):
                    for i in range(4):
                        mm = pe.transpose(bank[0:EXPERTS, 2 + g % 2, i * P:(i + 1) * P], cw[:, 4 * g + i, :], ident[:, :])
                    mm.then_inc(s_ct, 1)
                    if g >= 1:
                        pe.wait_ge(s_cto, g)
                for g in range(4):
                    pe.wait_ge(s_cto, g + 1)
                    for i in range(4):
                        mm = pe.matmul(bank[:, 4 + g, i * P:(i + 1) * P], cw_t[:, 4 * g + i, :], b2[:, :], start=True, stop=True)
                    mm.then_inc(s_b2, 1)

            @block.scalar
            def _(act):
                for b in range(B):
                    act.copy(h_high[:, b, :], h_in[:, b, PAD:PAD + N]).then_inc(s_high, 1)
                act.wait_ge(s_w, 48)
                split_high(act, 0, s_high)
                act.wait_ge(s_diff, 1)
                act.activation(wt[:, 1, :], wt[:, 0, :], ACT.Exp).then_inc(s_exp, 1)

            @block.vector
            def _(dve):
                for b in range(B):
                    dve.tensor_scalar(gb_diag[:, b, :], ident[:, :], mod[:, 1, 5, b:b + 1], None, ALU.mult).then_inc(s_gb, 1)
                dve.wait_ge(s_lg, 1)
                dve.tensor_copy(logits[:, :, :].rearrange("p t e -> p (t e)"), bank[:, 0, 0:TB * EXPERTS]).then_inc(s_lo, 1)
                dve.wait_ge(s_lo, 1)
                for t in range(TB):
                    dve.max(top[:, t, :], logits[:, t, :]).then_inc(s_top, 1)
                dve.wait_ge(s_top, TB)
                for t in range(TB):
                    dve.max_index(top_i[:, t, :], top[:, t, :], logits[:, t, :]).then_inc(s_idx, 1)
                dve.tensor_tensor(wt[:, 0, :], top[:, :, 1], top[:, :, 0], ALU.subtract).then_inc(s_diff, 1)
                dve.wait_ge(s_idx, TB)
                dve.tensor_copy(top_f[:, :, :], top_i[:, :, :]).then_inc(s_idf, 1)
                dve.wait_ge(s_idf, 1)
                dve.wait_ge(s_in, 48)
                for k in range(2):
                    dve.tensor_tensor(pick[:, k, :, :], top_f[:, :, k:k + 1].to_broadcast([P, TB, EXPERTS]),
                                      iota[:, :].unsqueeze(1).to_broadcast([P, TB, EXPERTS]), ALU.is_equal).then_inc(s_idf, 1)
                dve.wait_ge(s_exp, 1)
                dve.tensor_scalar(wt[:, 2, :], wt[:, 1, :], 1.0, None, ALU.add).then_inc(s_wt, 1)
                dve.wait_ge(s_wt, 1)
                dve.reciprocal(wt[:, 2, :], wt[:, 2, :]).then_inc(s_wt, 1)
                dve.wait_ge(s_wt, 2)
                dve.tensor_tensor(wt[:, 3, :], wt[:, 1, :], wt[:, 2, :], ALU.mult).then_inc(s_wt, 1)
                dve.wait_ge(s_wt, 3)
                dve.wait_ge(s_idf, 3)
                for k in range(2):
                    dve.tensor_tensor(pick[:, k, :, :], pick[:, k, :, :],
                                      wt[:, 2 + k, :].unsqueeze(2).to_broadcast([P, TB, EXPERTS]), ALU.mult).then_inc(s_cw, 1)
                dve.wait_ge(s_cw, 2)
                dve.tensor_tensor(cw[:, :, :], pick[:, 0, :, :], pick[:, 1, :, :], ALU.add).then_inc(s_cw, 1)
                dve.wait_ge(s_gbm, 1)
                dve.tensor_copy(gb_all[:, :, :].rearrange("p b d -> p (b d)"), bank[:, 1, 0:B * P]).then_inc(s_gbo, 1)
                for g in range(4):
                    dve.wait_ge(s_ct, g + 1)
                    dve.tensor_copy(cw_t[:, 4 * g:4 * g + 4, :].rearrange("e t n -> e (t n)"), bank[0:EXPERTS, 2 + g % 2, :])\
                       .then_inc(s_cto, 1)
                for g in range(4):
                    dve.wait_ge(s_b2, g + 1)
                    dve.tensor_copy(acc[:, 4 * g:4 * g + 4, :].rearrange("p t d -> p (t d)"), bank[:, 4 + g, :]).then_inc(s_b2o, 1)
                dve.wait_ge(s_b2o, 4)
                dve.wait_ge(s_gbo, 1)

        names = "odd next high low cw_e up gelu down added".split()
        first = {n: sem(f"s_ex_{n}", ctx) for n in names}
        S = type("S", (), first)
        numbers = [s.num for s in first.values()]
        span = range(min(numbers), max(numbers) + 1)
        def chunk(t, c):
            return t[:, c // 2, (c % 2) * CH:(c % 2 + 1) * CH]

        with nc.Fori(0, EXPERTS // 2) as two:
            e = 2 * two
            with nc.Block(no_gpsimd_drain=True) as block:
                @block.sync
                def _(sp):
                    sp.dma_start(w1[:, 1, :], A["ex_w1"][e + 1]).then_inc(S.odd, 16)
                    sp.dma_start(w2[:, 1, :, :], A["ex_w2"][e + 1]).then_inc(S.odd, 16)
                    sp.dma_start(b1[:, 1, :], A["ex_b1"][e + 1]).then_inc(S.odd, 16)
                    sp.wait_ge(S.odd, 48)
                    sp.wait_ge(S.down, NCH)
                    sp.dma_start(w1[:, 0, :], A["ex_w1"][e + 2]).then_inc(S.next, 16)
                    sp.dma_start(w2[:, 0, :, :], A["ex_w2"][e + 2]).then_inc(S.next, 16)
                    sp.dma_start(b1[:, 0, :], A["ex_b1"][e + 2]).then_inc(S.next, 16)
                    sp.wait_ge(S.next, 48)

                @block.gpsimd
                def _(pool):
                    for i, k in enumerate((1, 0)):
                        pool.wait_ge(S.high, i + 1)
                        split_low(pool, k, S.low)
                    pool.wait_ge(S.low, 2)

                @block.tensor
                def _(pe):
                    def up(n):
                        k, c = n // NCH, n % NCH
                        if n == NCH:
                            pe.wait_ge(S.odd, 48)
                            pe.wait_ge(S.low, 1)
                        for j in range(EFB):
                            if n >= 1:
                                pe.wait_ge(S.gelu, EFB * (n - 1) + j + 1)
                            col = slice(j * P, (j + 1) * P)
                            pe.matmul(bank[:, j, :], w1_high[:, k, col], chunk(h_high, c), start=True, stop=False)
                            pe.matmul(bank[:, j, :], w1_high[:, k, col], chunk(h_low, c), start=False, stop=False)
                            pe.matmul(bank[:, j, :], w1_low[:, k, col], chunk(h_high, c), start=False, stop=True)\
                              .then_inc(S.up, 1)

                    def down(n):
                        k, c = n // NCH, n % NCH
                        pe.wait_ge(S.gelu, EFB * (n + 1))
                        if n >= 2:
                            pe.wait_ge(S.added, 4 * (n - 1))
                        for t in range(4):
                            for j in range(EFB):
                                mm = pe.matmul(bank[:, 4 + n % 2, t * P:(t + 1) * P], hid[:, n % 2, j, t * P:(t + 1) * P],
                                               w2[:, k, j, :], start=j == 0, stop=j == EFB - 1)
                        mm.then_inc(S.down, 1)

                    for n in range(2 * NCH):
                        up(n)
                        if n >= 1:
                            down(n - 1)
                    down(2 * NCH - 1)

                @block.scalar
                def _(act):
                    for n in range(2 * NCH):
                        if n == NCH:
                            act.wait_ge(S.odd, 48)
                        for j in range(EFB):
                            act.wait_ge(S.up, EFB * n + j + 1)
                            if n >= 2 and j == 0:
                                act.wait_ge(S.down, n - 1)
                            act.activation(hid[:, n % 2, j, :], bank[:, j, :], ACT.Gelu, bias=b1[:, n // NCH, j:j + 1])\
                               .then_inc(S.gelu, 1)
                        if n == 1:
                            act.wait_ge(S.odd, 48)
                            split_high(act, 1, S.high)
                        elif n == 2 * NCH - 2:
                            act.wait_ge(S.next, 48)
                            split_high(act, 0, S.high)

                @block.vector
                def _(dve):
                    for k in range(2):
                        dve.tensor_copy(cw_e[:, k, :], cw[:, :, e + k]).then_inc(S.cw_e, 1)
                    dve.wait_ge(S.cw_e, 2)
                    for n in range(2 * NCH):
                        k, c = n // NCH, n % NCH
                        dve.wait_ge(S.down, n + 1)
                        if n == NCH:
                            dve.wait_ge(S.added, 4 * NCH)
                        for t in range(4):
                            a = acc[:, 4 * c + t, :]
                            dve.scalar_tensor_tensor(out=a, in0=bank[:, 4 + n % 2, t * P:(t + 1) * P],
                                                     scalar=cw_e[:, k, 4 * c + t:4 * c + t + 1], in1=a,
                                                     op0=ALU.mult, op1=ALU.add).then_inc(S.added, 1)
                    dve.wait_ge(S.added, 8 * NCH)

            nc.all_engine_barrier(sems_to_clear=span)

        s_xt = sem("s_ex_x_turned")
        s_gy = sem("s_ex_gated")
        s_y = sem("s_ex_y")
        s_out = sem("s_ex_out")
        rows = out.rearrange("b (t p) d -> p (b t) d", p=P)
        with nc.Block() as block:
            @block.tensor
            def _(pe):
                for g in range(4):
                    for i in range(4):
                        t = 4 * g + i
                        mm = pe.transpose(bank[:, g, i * P:(i + 1) * P],
                                          x_main[:, t // 8, (t % 8) * P:(t % 8 + 1) * P], ident[:, :])
                    mm.then_inc(s_xt, 1)

            @block.vector
            def _(dve):
                for g in range(4):
                    o = y[:, 4 * g:4 * g + 4, :]
                    dve.tensor_tensor(o, acc[:, 4 * g:4 * g + 4, :], gb_all[:, g // 2:g // 2 + 1, :].to_broadcast([P, 4, P]),
                                      ALU.mult).then_inc(s_gy, 1)
                    dve.wait_ge(s_gy, g + 1)
                    dve.wait_ge(s_xt, g + 1)
                    dve.tensor_tensor(o, o, bank[:, g, :].rearrange("p (t d) -> p t d", d=P), ALU.add).then_inc(s_y, 1)

            @block.sync
            def _(sp):
                for g in range(4):
                    sp.wait_ge(s_y, g + 1)
                    sp.dma_start(rows[:, 4 * g:4 * g + 4, :], y[:, 4 * g:4 * g + 4, :]).then_inc(s_out, 16)
                sp.wait_ge(s_out, 64)


def _constants():
    import numpy as np
    f = np.float32
    half = np.arange(0, HD, 2, dtype=f)
    inv_freq = (f(1.0) / np.power(f(10000.0), half / f(HD))).astype(f)
    t = np.arange(N, dtype=f)
    freqs = t[:, None] * inv_freq[None, :]
    base = (half + f(0.4 * HD)) / f(1.4 * HD)
    power = (t - f(N // 2)) / f(WIN // 2)
    scale = np.power(base[None, :], power[:, None]).astype(f)
    qk = np.stack([scale * f(8.0), f(1.0) / scale], 1)
    cos = np.cos(freqs)[:, None, :] * qk
    sin = np.sin(freqs)[:, None, :] * qk
    cos = np.concatenate([cos, cos], -1).astype(f)
    sin = np.concatenate([-sin, sin], -1).astype(f)

    def blocks(a):
        return np.ascontiguousarray(a.reshape(N // P, P, 2 * HD).transpose(1, 0, 2))

    q = np.arange(P)
    key = np.arange(HD)
    i, w = q % WIN, q // WIN
    allowed = np.where(key[None, :] < WIN, key[None, :] >= i[:, None], key[None, :] - WIN <= i[:, None])
    start = allowed & ~((w[:, None] == 0) & (key[None, :] < WIN))
    mask = np.where(np.stack([start, allowed], 1), f(0), f(-1e30)).astype(f)
    eye = np.eye(P, dtype=f)
    return {
        "cos": blocks(cos), "sin": blocks(sin), "mask": mask, "ident": eye,
        "anti": np.ascontiguousarray(eye[::-1]),
        "group_mean": np.kron(np.eye(P // 8, dtype=f), np.full((8, 8), 0.125, f)).astype(f),
        "iota": np.tile(np.arange(EXPERTS, dtype=f), (P, 1)),
    }


def _layout(d):
    import numpy as np
    c = np.ascontiguousarray

    def cat(*a):
        return c(np.stack(a, 1))

    def again(a):
        return c(np.concatenate([a, a[-1:]], 0))

    L = d
    wqkv = L["L0_ffn_Wqkv"]
    wv = wqkv[..., 2 * INNER:].reshape(LAYERS, P, PAIRS, 2, HD).transpose(0, 1, 3, 2, 4).reshape(LAYERS, P, INNER)
    lv = np.zeros((LAYERS, P, 9), np.float32)
    lv[:, :, 0], lv[:, :, 1], lv[:, :, 2] = L["L0_ffn_ln_g"], L["L0_ffn_ln_b"], L["L0_ffn_b2"]
    b1 = L["L0_ffn_b1"]
    w2 = np.zeros((LAYERS, P, FB, P), np.float32)
    for j in range(FB):
        m = FROWS[j]
        lv[:, 0:m, 3 + j] = b1[:, j * P:j * P + m]
        lv[:, 0:m, 6 + j] = b1[:, FF + j * P:FF + j * P + m]
        w2[:, 0:m, j, :] = L["L0_ffn_W2"][:, j * P:j * P + m, :]
    rel = L["L1_attn_rel_bias"].T
    rel = np.concatenate([rel, np.repeat(rel[:, -1:], 384 - rel.shape[1], 1)], 1)
    hankel = rel[:, np.arange(P)[:, None] + np.arange(2 * P)]
    w = L["L1_attn_w_qkv"].reshape(HD, 3, PAIRS, 2, P)
    return {
        "x_t": c(L["L0_attn_x"].transpose(2, 0, 1)),
        "c_t": c(np.stack([L["L0_c"].T, L["L1_c"].T], 1)),
        "wmod": cat(L["L0_wmod"], L["L1_wmod"]),
        "tm_w": cat(*[L[f"L0_attn_W{n}_w"].T for n in "grkvo"]),
        "tm_vec": cat(*[L[f"L0_attn_W{n}_b"] for n in "grkvo"], *[L[f"L0_attn_m{n}"] for n in "grkv"],
                      L["L0_attn_w"].reshape(-1), L["L0_attn_u"].reshape(-1)),
        "lt_wqkv": again(np.concatenate([wqkv[..., :2 * INNER], wv], -1)),
        "lt_qkscale": again(np.concatenate([L["L0_ffn_q_scale"], L["L0_ffn_k_scale"]], 1)[:, None, :]),
        "lt_wo": c(L["L0_ffn_Wo"].reshape(LAYERS, PAIRS, P, P).transpose(0, 2, 1, 3)),
        "lt_w1": c(L["L0_ffn_W1"]), "lt_w2": w2, "lt_vec": lv,
        "fa_w": again(w.transpose(2, 4, 1, 3, 0).reshape(PAIRS, P, 3, P)),
        "fa_rel": c(hankel.reshape(PAIRS, 2, P, 2 * P).transpose(0, 2, 1, 3)),
        "fa_wout": c(L["L1_attn_w_out"].T.reshape(PAIRS, P, P)),
        "gate_w": c(L["L1_ffn_gate_w"]), "ex_b2": c(L["L1_ffn_b2"]),
        "ex_w1": again(L["L1_ffn_w1"]),
        "ex_w2": again(L["L1_ffn_w2"].reshape(EXPERTS, EFB, P, P).transpose(0, 2, 1, 3)),
        "ex_b1": again(L["L1_ffn_b1"].reshape(EXPERTS, EFB, P).transpose(0, 2, 1)),
    }


def kernel(**inputs):
    import numpy as _np
    import concourse.bacc as _bacc
    from concourse import mybir as _mybir
    from concourse.bass_utils import run_bass_kernel_spmd as _run

    nc = _bacc.Bacc("TRN2", target_bir_lowering=False, num_devices=1)
    host = {**_layout({k: _np.asarray(v) for k, v in inputs.items()}), **_constants()}
    arrays, aps = {}, {}
    for name, a in host.items():
        arrays[f"in_{name}_dram"] = _np.ascontiguousarray(a)
        aps[name] = nc.dram_tensor(f"in_{name}_dram", a.shape, _mybir.dt.from_np(a.dtype), kind="ExternalInput").ap()
    o = nc.dram_tensor("out_0_dram", (B, N, P), F32, kind="ExternalOutput").ap()
    build(nc, aps, o)
    r = _run(nc, [arrays], core_ids=[0])
    return r.results[0]["out_0_dram"]
```
